# Optimizing a Trainium2 kernel written in Bass

```python
import numpy as np
import jax
import jax.numpy as jnp

def _softmax(x, axis=-1):
    return jax.nn.softmax(x, axis=axis)

def _gelu(x):
    return jax.nn.gelu(x, approximate=True)

def _silu(x):
    return jax.nn.silu(x)

def _sigmoid(x):
    return jax.nn.sigmoid(x)

def _layernorm(x, axis=-1, eps=1e-05):
    m = jnp.mean(x, axis=axis, keepdims=True)
    v = jnp.var(x, axis=axis, keepdims=True)
    return (x - m) / jnp.sqrt(v + eps)

def _scatter_add(tgt, idx, src, axis=0):
    return tgt.at[idx].add(src)

def _segment_sum(src, seg, n):
    return jax.ops.segment_sum(src, seg, n)
kernel_name = 'mk_cond_resid_d2_seqx_r8_608aa7'

def setup_inputs(seed: int=0):
    np.random.seed(seed)
    _w = jnp.asarray

    def _rec_inputs():
        import jax
        import jax.numpy as jnp
        _rk = jax.random.key(seed)
        x = 7.22e-05 + 1 * jax.random.normal(jax.random.fold_in(_rk, 1), (32, 32, 512), jnp.float32)
        _lenS = 32 - jax.random.randint(jax.random.fold_in(_rk, 7), (32,), 0, max(1, 32 // 4) + 1, jnp.int32)
        _lenS2 = 32 - jax.random.randint(jax.random.fold_in(_rk, 8), (32,), 0, max(1, 32 // 4) + 1, jnp.int32)
        itok_B_2_6 = jax.random.randint(jax.random.fold_in(_rk, 11), (32,), 2, 7, jnp.int32)
        itok_B_8_3872 = jax.random.randint(jax.random.fold_in(_rk, 12), (32,), 8, 3873, jnp.int32)
        return (x, itok_B_2_6, itok_B_8_3872)
    x, itok_B_2_6, itok_B_8_3872 = _rec_inputs()

    def _L0_cond_setup():
        import jax, jax.numpy as jnp
        import numpy as np
        B, N, H, F = (4, 64, 512, 1376)
        L, R, RANK = (1, 16, 16)
        SCALE = 0.5
        key = jax.random.key(seed)
        ks = jax.random.split(key, 12)
        nrm = lambda k, shape, fan: jax.random.normal(k, shape, jnp.float32) * fan ** (-0.5)
        inp = {'x': jax.random.normal(ks[0], (B, N, H), jnp.float32), 'W_gate': nrm(ks[1], (F, H), H), 'W_up': nrm(ks[2], (F, H), H), 'W_down': nrm(ks[3], (H, F), F), 'A_gate': nrm(ks[4], (L, R, RANK, H), H), 'B_gate': nrm(ks[5], (L, R, F, RANK), RANK), 'A_up': nrm(ks[6], (L, R, RANK, H), H), 'B_up': nrm(ks[7], (L, R, F, RANK), RANK), 'A_down': nrm(ks[8], (L, R, RANK, F), F), 'B_down': nrm(ks[9], (L, R, H, RANK), RANK), 'lora_indices': jax.random.randint(ks[10], (B,), 0, R), 'layer_idx': 0}
        return inp
    _L0_cond_all = _L0_cond_setup()
    _L0_cond_in = {k: v for k, v in _L0_cond_all.items() if k in ('W_gate', 'W_up', 'W_down', 'A_gate', 'B_gate', 'A_up', 'B_up', 'A_down', 'B_down')}
    del _L0_cond_all

    def _L1_cond_setup():
        import math
        import jax, jax.numpy as jnp
        import numpy as np
        H, N, B, L = (32, 64, 16, 512)
        DT_MIN, DT_MAX = (0.001, 0.1)

        def _get_kernel(log_dt, C, log_A_real, A_imag, length):
            Cc = C[..., 0] + 1j * C[..., 1]
            dt = jnp.exp(log_dt)
            A = -jnp.exp(log_A_real) + 1j * A_imag
            dtA = A * dt[:, None]
            P = dtA[:, :, None] * jnp.arange(length, dtype=jnp.float32)
            Cs = Cc * (jnp.exp(dtA) - 1.0) / A
            K = 2.0 * jnp.einsum('hn,hnl->hl', Cs, jnp.exp(P)).real
            return K
        key = jax.random.key(seed)
        ks = jax.random.split(key, 6)
        u = jax.random.normal(ks[0], (B, H, L), dtype=jnp.float32)
        length = jax.random.randint(ks[1], (B,), 0, L)
        log_dt = jax.random.uniform(ks[2], (H,), dtype=jnp.float32) * (math.log(DT_MAX) - math.log(DT_MIN)) + math.log(DT_MIN)
        C = jax.random.normal(ks[3], (H, N, 2), dtype=jnp.float32)
        log_A_real = jnp.log(0.5 * jnp.ones((H, N), dtype=jnp.float32))
        A_imag = math.pi * jnp.broadcast_to(jnp.arange(N, dtype=jnp.float32), (H, N))
        D = jax.random.normal(ks[4], (H,), dtype=jnp.float32)
        return {'u': u, 'length': length, 'log_dt': log_dt, 'C': C, 'log_A_real': log_A_real, 'A_imag': A_imag, 'D': D}
    _L1_cond_all = _L1_cond_setup()
    _L1_cond_in = {k: v for k, v in _L1_cond_all.items() if k in ('log_dt', 'C', 'log_A_real', 'A_imag', 'D')}
    del _L1_cond_all
    return {'x': x, 'itok_B_2_6': itok_B_2_6, 'itok_B_8_3872': itok_B_8_3872, 'L0_cond_W_gate': _L0_cond_in['W_gate'], 'L0_cond_W_up': _L0_cond_in['W_up'], 'L0_cond_W_down': _L0_cond_in['W_down'], 'L0_cond_A_gate': _L0_cond_in['A_gate'], 'L0_cond_B_gate': _L0_cond_in['B_gate'], 'L0_cond_A_up': _L0_cond_in['A_up'], 'L0_cond_B_up': _L0_cond_in['B_up'], 'L0_cond_A_down': _L0_cond_in['A_down'], 'L0_cond_B_down': _L0_cond_in['B_down'], 'L1_cond_log_dt': _L1_cond_in['log_dt'], 'L1_cond_C': _L1_cond_in['C'], 'L1_cond_log_A_real': _L1_cond_in['log_A_real'], 'L1_cond_A_imag': _L1_cond_in['A_imag'], 'L1_cond_D': _L1_cond_in['D']}

def reference(x, itok_B_2_6, itok_B_8_3872, L0_cond_W_gate, L0_cond_W_up, L0_cond_W_down, L0_cond_A_gate, L0_cond_B_gate, L0_cond_A_up, L0_cond_B_up, L0_cond_A_down, L0_cond_B_down, L1_cond_log_dt, L1_cond_C, L1_cond_log_A_real, L1_cond_A_imag, L1_cond_D):
    import jax
    import jax.numpy as jnp

    def _L0_cond_ref(x, W_gate, W_up, W_down, A_gate, B_gate, A_up, B_up, A_down, B_down, lora_indices, layer_idx):
        import jax, jax.numpy as jnp
        import numpy as np
        B, N, H, F = (4, 64, 512, 1376)
        L, R, RANK = (1, 16, 16)
        SCALE = 0.5

        def lora_add(base, inp, A, B):
            Ab = A[layer_idx][lora_indices]
            Bb = B[layer_idx][lora_indices]
            t = jnp.einsum('bri,bni->bnr', Ab, inp)
            return base + jnp.einsum('bor,bnr->bno', Bb, t) * SCALE
        gate = lora_add(jnp.einsum('bnh,fh->bnf', x, W_gate), x, A_gate, B_gate)
        up = lora_add(jnp.einsum('bnh,fh->bnf', x, W_up), x, A_up, B_up)
        act = jax.nn.silu(gate) * up
        down = lora_add(jnp.einsum('bnf,hf->bnh', act, W_down), act, A_down, B_down)
        return down

    def _L1_cond_ref(u, length, log_dt, C, log_A_real, A_imag, D):
        import math
        import jax, jax.numpy as jnp
        import numpy as np
        H, N, B, L = (32, 64, 16, 512)
        DT_MIN, DT_MAX = (0.001, 0.1)

        def _get_kernel(log_dt, C, log_A_real, A_imag, length):
            Cc = C[..., 0] + 1j * C[..., 1]
            dt = jnp.exp(log_dt)
            A = -jnp.exp(log_A_real) + 1j * A_imag
            dtA = A * dt[:, None]
            P = dtA[:, :, None] * jnp.arange(length, dtype=jnp.float32)
            Cs = Cc * (jnp.exp(dtA) - 1.0) / A
            K = 2.0 * jnp.einsum('hn,hnl->hl', Cs, jnp.exp(P)).real
            return K
        Bq, Hq, Lq = u.shape
        mask = (jnp.arange(Lq) < length[:, None]).astype(u.dtype)
        u_m = u * mask[:, None, :]
        kernel = _get_kernel(log_dt, C, log_A_real, A_imag, Lq)
        n = 2 * Lq
        k_f = jnp.fft.rfft(kernel, n=n)
        u_f = jnp.fft.rfft(u_m, n=n)
        y = jnp.fft.irfft(u_f * k_f, n=n)[..., :Lq]
        y = y + u_m * D[:, None]
        return y * mask[:, None, :]
    x = x + _L0_cond_ref(x, L0_cond_W_gate, L0_cond_W_up, L0_cond_W_down, L0_cond_A_gate, L0_cond_B_gate, L0_cond_A_up, L0_cond_B_up, L0_cond_A_down, L0_cond_B_down, itok_B_2_6, 0)
    x = x + _L1_cond_ref(x, itok_B_8_3872, L1_cond_log_dt, L1_cond_C, L1_cond_log_A_real, L1_cond_A_imag, L1_cond_D)
    return x

_drawn_inputs = setup_inputs


def setup_inputs(seed=0):
    import zlib

    import numpy as np

    out = dict(_drawn_inputs(seed))
    spreads = {'L1_cond_log_A_real': (-0.6931471824645996, 0.2)}
    factors = {}
    for name, (base, spread) in spreads.items():
        noise = np.random.default_rng([zlib.crc32(name.encode()), seed]).standard_normal(out[name].shape)
        drawn = base * np.exp(spread * noise) if base else spread * noise
        out[name] = jnp.asarray(drawn.astype(out[name].dtype))
    for name, factor in factors.items():
        out[name] = (out[name] * factor).astype(out[name].dtype)
    return out
```

```python
import math
from contextlib import ExitStack

import numpy as np

import concourse.bass as bass
from concourse import mybir
from concourse.alu_op_type import AluOpType as ALU

F32 = mybir.dt.float32
F32R = mybir.dt.float32r
I32 = mybir.dt.int32
ACT = mybir.ActivationFunctionType

P = 128
NB, NN, H, F = 32, 32, 512, 1376
WARM = 4
WD_FIRST = 3
RANK, NAD = 16, 16
LORA_SCALE = 0.5
FC = -(-F // P)
KC = H // P
GB = P // RANK
NG = NB // GB
GT = GB * NN
TOK = NB * NN
HT = TOK // 2
NPART = (FC + 1) // 2
MODES = 64
LA, LJ = 16, 32
PAD = P
QN = 4
NQ = 4
SBUF0 = 16512

C_J, C_PHE, C_PHU, C_PHV, C_RANK, C_BLOCK, C_POS = 0, 32, 34, 36, 38, 39, 47
NCONST = C_POS + KC

LOG2E = 1.0 / math.log(2.0)
LN2_HI, LN2_LO = 0.693145751953125, 1.42860676533018518e-06
INV_2PI = 1.0 / (2.0 * math.pi)
PI2_1 = 6.28125
PI2_2 = 2.0 * math.pi - PI2_1
PI_IN = 3.1415925
ROUND = 1.5 * 2.0 ** 23


def constants():
    c = np.zeros((P, NCONST), np.float32)
    p = np.arange(P)
    imag = p // MODES
    c[:, C_J:C_J + LJ] = np.arange(LJ)
    for col, turns in ((C_PHE, (0.25, 0.0)), (C_PHU, (0.25, 0.5)), (C_PHV, (0.0, 0.25))):
        c[:, col] = np.array(turns)[imag]
        c[:, col + 1] = np.array(turns)[imag] * 2.0 * math.pi
    c[:, C_RANK] = p % RANK
    c[:, C_BLOCK:C_BLOCK + GB] = LORA_SCALE * (p[:, None] // RANK == np.arange(GB))
    c[:, C_POS:C_POS + KC] = (P - 1 - p[:, None]) + P * np.arange(KC)
    return c


def program(nc, x_t, x_rev, w_gu, w_d, a_gu, a_d, b_gu, b_d, idx_row, ints, params, skip, consts, out):
    ctx = ExitStack()
    with ctx:
        def sem(name):
            return ctx.enter_context(nc.semaphore(name))

        def at(name, kib, shape, dt=F32):
            return nc.alloc_sbuf_tensor_at(name, shape, dt, offset=SBUF0 + int(kib * 1024))

        ctx.enter_context(nc.sbuf_tensor("slab", [P, (205 * 1024) // 4], F32))

        b_raw = at("b_raw", 0, [P, NPART, NG, 2 * 2 * P])
        x_raw = at("x_raw", 16, [P, KC, TOK])
        agu_raw = at("agu_raw", 32, [P, NB, 2 * KC * RANK])
        ad_raw = at("ad_raw", 0, [P, NB, FC * RANK])
        ad_hi = [at(f"ad_hi{s}", 24 + 4 * s, [P, NB * RANK], F32R) for s in range(2)]
        ad_lo = [at(f"ad_lo{s}", 26 + 4 * s, [P, NB * RANK], F32R) for s in range(2)]
        toep = [at(f"toep{q}", 8 * q, [P, QN, H]) for q in range(NQ)]
        b_hi = [at(f"b_hi{s}", 56 - 8 * s, [P, NG, 2 * P], F32R) for s in range(2)]
        b_lo = [at(f"b_lo{s}", 60 - 8 * s, [P, NG, 2 * P], F32R) for s in range(2)]
        w_hi = [at(f"w_hi{s}", 64 + 8 * s, [P, 2 * KC, P], F32R) for s in range(2)]
        w_lo = [at(f"w_lo{s}", 68 + 8 * s, [P, 2 * KC, P], F32R) for s in range(2)]
        w_raw = [at(f"w_raw{s}", 80 + 4 * s, [P, 2 * KC, P]) for s in range(2)]
        ha_hi = [at("ha_hi0", 72, [P, 2, HT], F32R), at("ha_hi1", 56, [P, 2, HT], F32R)]
        ha_lo = [at("ha_lo0", 76, [P, 2, HT], F32R), at("ha_lo1", 60, [P, 2, HT], F32R)]
        hb_hi = [at(f"hb_hi{s}", 64 + 4 * s, [P, HT], F32R) for s in range(2)]
        hb_lo = [at(f"hb_lo{s}", 66 + 4 * s, [P, HT], F32R) for s in range(2)]
        wd_raw = at("wd_raw", 32, [P, FC, H])
        trev = [at(f"trev{s}", 130 + 8 * s, [P, QN, H]) for s in range(2)]
        conv_tmp = [at(f"conv_tmp{s}", 80 + 2 * s, [P, QN, KC * NB]) for s in range(2)]
        t_mask = at("t_mask", 88, [P, 2, TOK])
        silu = [at(f"silu{s}", 88 + 4 * s, [P, TOK]) for s in range(2)]
        td_mask = at("td_mask", 88, [P, TOK])
        k_sb = at("k_sb", 92, [LA, NN, LJ])
        ssm_e = at("ssm_e", 96, [P, NN, LJ])
        ssm_g = at("ssm_g", 100, [P, NN, LA])
        hid = at("hid", 102, [P, 2, FC * HT])
        agu_hi = [at(f"agu_hi{g}", 102 + 8 * g, [P, 2 * KC, P], F32R) for g in range(NG)]
        agu_lo = [at(f"agu_lo{g}", 106 + 8 * g, [P, 2 * KC, P], F32R) for g in range(NG)]
        ang = at("ang", 134, [P, NN * LJ])
        turn = at("turn", 138, [P, NN * LJ])
        amp = at("amp", 142, [P, NN * LJ])
        x1 = at("x1", 102, [P, NN, KC, NB])
        x_hi = at("x_hi", 146, [P, KC, TOK], F32R)
        x_lo = at("x_lo", 162, [P, KC, TOK], F32R)
        td_hi = at("td_hi", 146, [P, TOK], F32R)
        td_lo = at("td_lo", 150, [P, TOK], F32R)
        bd_raw = at("bd_raw", 154, [P, NG, H])
        bd_hi = at("bd_hi", 162, [P, NG, H], F32R)
        bd_lo = at("bd_lo", 170, [P, NG, H], F32R)
        t_hi = at("t_hi", 178, [P, 2, TOK], F32R)
        t_lo = at("t_lo", 186, [P, 2, TOK], F32R)
        x_res = at("x_res", 178, [P, KC, TOK])
        sm = at("sm", 194, [P, 40, NN])
        wd_hi = [at(f"wd_hi{s}", 194 + 4 * s, [P, H], F32R) for s in range(2)]
        wd_lo = [at(f"wd_lo{s}", 196 + 4 * s, [P, H], F32R) for s in range(2)]
        cst = at("cst", 202, [P, NCONST])
        ints_sb = at("ints_sb", 202.25, [P, NB + NG], I32)
        idx_sb = at("idx_sb", 202.5, [1, NB], I32)
        skip_sb = at("skip_sb", 202.75, [1, NN])
        rows_f = at("rows_f", 203, [P, NG])
        rows = at("rows", 203.125, [P, NPART + 1, NG], I32)
        mask = at("mask", 203.25, [P, KC, NB])
        lens_f = at("lens_f", 203.75, [P, NB])
        zeros = at("zeros", 204, [NN, PAD])
        junk = at("junk", 204.5, [NN, 1])
        ang_g = at("ang_g", 114, [P, 2 * NN * LA])
        turn_g = at("turn_g", 118, [P, 2 * NN * LA])
        warm = at("warm", 56, [P, HT])
        amp_g = at("amp_g", 199, [P, NN * LA])

        banks = ctx.enter_context(nc.psum_tensor("banks", [P, 8, HT], F32))

        k_pad = nc.dram_tensor("k_pad", (NN, PAD + H), F32, kind="Internal").ap()

        d_small = sem("d_small")
        d_idx = sem("d_idx")
        d_x = [sem(f"d_x{k}") for k in range(KC)]
        d_w = [sem(f"d_w{s}") for s in range(2)]
        d_agu = [sem(f"d_agu{g}") for g in range(NG)]
        d_b = sem("d_b")
        d_ad = sem("d_ad")
        d_bd = sem("d_bd")
        d_wd = [sem(f"d_wd{s}") for s in range(2)]
        d_xres = sem("d_xres")
        d_kpad = sem("d_kpad")
        d_t = [sem(f"d_t{q}") for q in range(NQ)]
        d_out = sem("d_out")
        idx_ready = sem("idx_ready")
        zeros_ready = sem("zeros_ready")
        warm_ready = sem("warm_ready")
        warm_used = sem("warm_used")
        xh_done = sem("xh_done")
        xl_done = sem("xl_done")
        aguh_done = sem("aguh_done")
        agul_done = sem("agul_done")
        la_done = sem("la_done")
        tm_done = sem("tm_done")
        th_done = sem("th_done")
        tl_done = sem("tl_done")
        wh_done = sem("wh_done")
        wl_done = sem("wl_done")
        bh_done = sem("bh_done")
        bl_done = sem("bl_done")
        w_used = sem("w_used")
        gu_done = sem("gu_done")
        silu_done = sem("silu_done")
        hid_done = sem("hid_done")
        hh_done = sem("hh_done")
        hl_done = sem("hl_done")
        wdh_done = sem("wdh_done")
        wdl_done = sem("wdl_done")
        adh_done = sem("adh_done")
        adl_done = sem("adl_done")
        down_used = sem("down_used")
        td_done = sem("td_done")
        tdm_done = sem("tdm_done")
        tdh_done = sem("tdh_done")
        tdl_done = sem("tdl_done")
        bdh_done = sem("bdh_done")
        bdl_done = sem("bdl_done")
        y_done = sem("y_done")
        x1_done = sem("x1_done")
        bank_free = sem("bank_free")
        conv_done = sem("conv_done")
        rev_done = sem("rev_done")
        out_ready = sem("out_ready")
        k_mm = sem("k_mm")
        k_ready = sem("k_ready")
        dve_chain = sem("dve_chain")
        pool_chain = sem("pool_chain")
        s_rates = sem("s_rates")
        s_exp1 = sem("s_exp1")
        s_cs = sem("s_cs")
        s_ampin = sem("s_ampin")
        s_amp = sem("s_amp")
        s_ang = sem("s_ang")
        s_sin = sem("s_sin")
        s_e = sem("s_e")

        block = ctx.enter_context(nc.Block())

        def spread(ap, dims):
            return bass.AP(tensor=ap.tensor, offset=ap.offset, ap=[list(ap.ap[0])] + dims)

        names = ("are dt x_ k_ r_ p_ s_ ai cr ci ar th r1 ra ea tnh sh sn em cm zre zim den rden "
                 "q1 q2 q3 q4 sre sim ar32 hk ldt lar").split()
        slot = {}
        for i, n_ in enumerate(["ldt", "lar", "ai", "cr", "ci", "k0", "k1", "r0", "r_1", "p0", "p1", "e0", "e1",
                                "dt", "are"] + [n for n in names if n not in ("ldt", "lar", "ai", "cr", "ci", "dt",
                                                                            "are", "x_", "k_", "r_", "p_", "s_")]):
            slot[n_] = i

        def small(name, width=1):
            return sm[:, slot[name]:slot[name] + width, :].rearrange("p a b -> p (a b)")

        def c_col(i):
            return cst[:, i:i + 1]

        @block.sync
        def _(sp):
            def load_toeplitz(q, turn_):
                first = k_pad[0:1, 0:1]
                src = bass.AP(tensor=first.tensor, offset=(turn_ * NQ + q) * QN * (PAD + H) + PAD - (P - 1),
                              ap=[[1, P], [PAD + H, QN], [1, H]])
                sp.dma_start(toep[q][:], src).then_inc(d_t[q], 16)

            sp.dma_start(x_raw[:, 0, :], x_t[:, 0, :]).then_inc(d_x[0], 16)
            sp.dma_start(w_raw[0][:], w_gu[0]).then_inc(d_w[0], 16)
            sp.dma_start(idx_sb[:], idx_row).then_inc(d_idx, 16)
            for k in range(1, KC):
                sp.dma_start(x_raw[:, k, :], x_t[:, k, :]).then_inc(d_x[k], 16)
            sp.wait_ge(d_idx, 16)
            for g in (0, 2, 3):
                _, ads = nc.values_load_multi_w_load_instructions(
                    idx_sb[0:1, g * GB:(g + 1) * GB], engines=[mybir.EngineType.SP], min_val=0, max_val=NAD - 1,
                    skip_runtime_bounds_check_because="an adaptor's index")
                for i, ad in enumerate(ads):
                    sp.dma_start(agu_raw[:, g * GB + i:g * GB + i + 1, :],
                                 a_gu[bass.ds(ad, 1), :, :].rearrange("o p c -> p o c")).then_inc(d_agu[g], 16)
                if g == 0:
                    sp.dma_start(ints_sb[:], ints).then_inc(d_small, 16)
                    sp.dma_start(cst[:], consts).then_inc(d_small, 16)
                    sp.dma_start(sm[:, 0:5, :].rearrange("p a b -> p (a b)"), params).then_inc(d_small, 16)
                    sp.dma_start(skip_sb[:], skip).then_inc(d_small, 16)
            sp.dma_start(w_raw[1][:], w_gu[1]).then_inc(d_w[1], 16)

            def load_w(j, s):
                sp.wait_ge(wh_done, j - 1)
                sp.wait_ge(wl_done, j - 1)
                sp.dma_start(w_raw[s][:], w_gu[bass.ds(j, 1)].rearrange("o p c f -> p (o c) f")).then_inc(d_w[s], 16)

            with sp.Fori(0, 3) as i:
                load_w(2 * i + 2, 0)
                load_w(2 * i + 3, 1)
            load_w(8, 0)
            sp.wait_ge(bh_done, 6)
            sp.wait_ge(bl_done, 6)
            with sp.Fori(0, NG) as g:
                _, ads = nc.values_load_multi_w_load_instructions(
                    idx_sb[0:1, bass.ds(g * GB, GB)], engines=[mybir.EngineType.SP], min_val=0, max_val=NAD - 1,
                    skip_runtime_bounds_check_because="an adaptor's index")
                for i, ad in enumerate(ads):
                    sp.dma_start(ad_raw[:, bass.ds(g * GB + i, 1), :],
                                 a_d[bass.ds(ad, 1), :, :].rearrange("o p c -> p o c")).then_inc(d_ad, 16)
            load_w(9, 1)
            load_w(10, 0)

            sp.wait_ge(bh_done, FC)
            sp.wait_ge(bl_done, FC)
            sp.wait_ge(gu_done, FC - 1)
            sp.dma_start(wd_raw[:, 0:WD_FIRST, :], w_d[:, 0:WD_FIRST, :]).then_inc(d_wd[0], 16)
            sp.dma_start(wd_raw[:, WD_FIRST:FC, :], w_d[:, WD_FIRST:FC, :]).then_inc(d_wd[1], 16)
            sp.wait_ge(gu_done, FC)
            sp.dma_start(x_res[:], x_rev).then_inc(d_xres, 16)
            sp.wait_ge(zeros_ready, 1)
            sp.dma_start(k_pad[:, 0:PAD], zeros[:]).then_inc(d_kpad, 16)
            sp.wait_ge(k_ready, 1)
            sp.dma_start(k_pad[:, PAD:PAD + H].rearrange("h (a j) -> a h j", j=LJ), k_sb[:]).then_inc(d_kpad, 16)
            sp.wait_ge(d_kpad, 32)
            sp.wait_ge(down_used, FC)
            for q in range(NQ):
                load_toeplitz(q, 0)
            for q in range(NQ):
                sp.wait_ge(rev_done, q + 1)
                load_toeplitz(q, 1)
            for t in range(2 * NQ):
                sp.wait_ge(out_ready, t + 1)
                sp.dma_start(out[:, t * QN:(t + 1) * QN, :],
                             x1[:, t * QN:(t + 1) * QN, :, :].rearrange("p n c b -> p n (c b)")).then_inc(d_out, 16)
            sp.wait_ge(d_out, 16 * 2 * NQ)

        @block.gpsimd
        def _(pool):
            chain = [0]

            def link(ins):
                chain[0] += 1
                ins.then_inc(pool_chain, 1)
                pool.wait_ge(pool_chain, chain[0])

            def gather_part(part):
                for g in range(NG):
                    nc.gpsimd.indirect_dma_start(
                        out=b_raw[:, part, g, :], out_offset=None, in_=b_gu,
                        in_offset=bass.IndirectOffsetOnAxis(ap=rows[:, part, g:g + 1], axis=0)).then_inc(d_b, 16)

            def split_w(j, s):
                pool.wait_ge(wh_done, j + 1)
                if not (isinstance(j, int) and j < 2):
                    pool.wait_ge(w_used, j - 1)
                nc.gpsimd.tensor_tensor(w_lo[s][:], w_raw[s][:], w_hi[s][:].bitcast(F32),
                                        ALU.subtract).then_inc(wl_done, 1)

            pool.wait_ge(d_idx, 16)
            _, ads = nc.values_load_multi_w_load_instructions(
                idx_sb[0:1, GB:2 * GB], engines=[mybir.EngineType.Pool], min_val=0, max_val=NAD - 1,
                skip_runtime_bounds_check_because="an adaptor's index")
            for i, ad in enumerate(ads):
                nc.gpsimd.dma_start(agu_raw[:, GB + i:GB + i + 1, :],
                                    a_gu[bass.ds(ad, 1), :, :].rearrange("o p c -> p o c")).then_inc(d_agu[1], 16)
            pool.wait_ge(idx_ready, 1)
            pool.wait_ge(d_agu[NG - 1], 16 * GB)
            gather_part(0)
            pool.wait_ge(d_b, 64)
            gather_part(1)
            pool.wait_ge(d_b, 128)
            pool.wait_ge(xh_done, KC)
            pool.wait_ge(xl_done, KC)
            pool.wait_ge(wl_done, 2)
            split_w(2, 0)
            gather_part(2)
            split_w(3, 1)
            pool.wait_ge(d_b, 64 * 3)
            gather_part(3)
            pool.wait_ge(s_rates, 1)
            nc.gpsimd.tensor_tensor(
                amp[:].rearrange("p (h j) -> p h j", j=LJ), spread(small("ar"), [[1, NN], [0, LJ]]),
                spread(cst[:, C_J:C_J + LJ], [[0, NN], [1, LJ]]), ALU.mult).then_inc(s_ampin, 1)
            nc.gpsimd.tensor_tensor(
                amp_g[:].rearrange("p (h a) -> p h a", a=LA), spread(small("ar32"), [[1, NN], [0, LA]]),
                spread(cst[:, C_J:C_J + LA], [[0, NN], [1, LA]]), ALU.mult).then_inc(s_ampin, 1)
            split_w(4, 0)
            pool.wait_ge(s_amp, 1)
            pool.wait_ge(s_sin, 1)
            nc.gpsimd.tensor_tensor(ssm_e[:].rearrange("p h j -> p (h j)"), turn[:], amp[:],
                                    ALU.mult).then_inc(s_e, 1)
            split_w(5, 1)
            pool.wait_ge(s_amp, 2)
            pool.wait_ge(s_sin, 2)
            pool.wait_ge(s_cs, 1)
            u_, v_ = turn_g[:, 0:NN * LA], turn_g[:, NN * LA:2 * NN * LA]
            weight = {n: spread(small(n), [[1, NN], [0, LA]]) for n in ("sre", "sim")}
            ha = "p (h a) -> p h a"
            link(nc.gpsimd.tensor_tensor(u_, u_, amp_g[:], ALU.mult))
            link(nc.gpsimd.tensor_tensor(v_, v_, amp_g[:], ALU.mult))
            link(nc.gpsimd.tensor_tensor(u_.rearrange(ha, a=LA), u_.rearrange(ha, a=LA), weight["sre"], ALU.mult))
            link(nc.gpsimd.tensor_tensor(v_.rearrange(ha, a=LA), v_.rearrange(ha, a=LA), weight["sim"], ALU.mult))
            nc.gpsimd.tensor_tensor(ssm_g[:].rearrange("p h a -> p (h a)"), u_, v_, ALU.subtract).then_inc(s_e, 1)
            for part in range(4, NPART):
                pool.wait_ge(d_b, 64 * part)
                gather_part(part)
                split_w(2 * part - 2, 0)
                split_w(2 * part - 1, 1)
            split_w(10, 0)

            def split_wd(u, j, s):
                pool.wait_ge(wdh_done, u + 1)
                if isinstance(u, int) and u < 2:
                    pool.wait_ge(s_e, 2)
                else:
                    pool.wait_ge(down_used, u - 1)
                nc.gpsimd.tensor_tensor(wd_lo[s][:], wd_raw[:, bass.ds(j, 1), :].rearrange("p o c -> p (o c)"), wd_hi[s][:].bitcast(F32),
                                        ALU.subtract).then_inc(wdl_done, 1)

            split_wd(0, 0, 0)
            pool.wait_ge(gu_done, FC)
            for g in range(NG):
                nc.gpsimd.indirect_dma_start(
                    out=bd_raw[:, g, :], out_offset=None, in_=b_d,
                    in_offset=bass.IndirectOffsetOnAxis(ap=rows[:, NPART, g:g + 1], axis=0)).then_inc(d_bd, 16)
            split_wd(1, 1, 1)
            split_wd(2, 2, 0)
            for g in range(NG):
                pool.wait_ge(bdh_done, g + 1)
                nc.gpsimd.tensor_tensor(bd_lo[:, g, :], bd_raw[:, g, :], bd_hi[:, g, :].bitcast(F32),
                                        ALU.subtract).then_inc(bdl_done, 1)
                split_wd(3 + g, 3 + g, (3 + g) % 2)
            with pool.Fori(0, 2) as i:
                split_wd(2 * i + 7, 2 * i + 7, 1)
                split_wd(2 * i + 8, 2 * i + 8, 0)
            with pool.Fori(0, 5) as i:
                split_wd(2 * i + FC, 2 * i, 1)
                split_wd(2 * i + FC + 1, 2 * i + 1, 0)
            split_wd(2 * FC - 1, FC - 1, 1)

        @block.scalar
        def _(act):
            act.wait_ge(zeros_ready, 1)
            nc.scalar.activation(junk[:], zeros[:, 0:1], ACT.Exp)

            def split_w(j, s):
                if isinstance(j, int):
                    act.wait_ge(d_w[s], 16 * (j // 2 + 1))
                if not (isinstance(j, int) and j < 2):
                    act.wait_ge(w_used, j - 1)
                nc.scalar.copy(w_hi[s][:], w_raw[s][:]).then_inc(wh_done, 1)

            def split_b(pair, s):
                act.wait_ge(d_b, 64 * (pair + 1))
                if not (isinstance(pair, int) and pair == 0):
                    act.wait_ge(gu_done, 2 * pair + s - 1)
                nc.scalar.copy(b_hi[s][:], b_raw[:, bass.ds(pair, 1), :, s * 2 * P:(s + 1) * 2 * P].rearrange(
                    "p o g c -> p (o g) c")).then_inc(bh_done, 1)

            def make_silu(j, s):
                act.wait_ge(gu_done, j + 1)
                if not (isinstance(j, int) and j < 2):
                    act.wait_ge(hid_done, j - 1)
                nc.scalar.activation(silu[s][:], banks[:, 4 * s:4 * s + 2, :].rearrange("p h t -> p (h t)"),
                                     ACT.Silu).then_inc(silu_done, 1)

            def split_x(k):
                act.wait_ge(d_x[k], 16)
                nc.scalar.copy(x_hi[:, k, :], x_raw[:, k, :]).then_inc(xh_done, 1)

            def split_agu(g):
                act.wait_ge(d_agu[g], 16 * GB)
                nc.scalar.copy(agu_hi[g][:].rearrange("p c (b r) -> p c b r", r=RANK),
                               agu_raw[:, g * GB:(g + 1) * GB, :].rearrange("p b (c r) -> p c b r", r=RANK),
                               ).then_inc(aguh_done, 1)

            split_x(0)
            split_w(0, 0)
            for k in range(1, KC):
                split_x(k)
            split_agu(0)
            split_agu(1)
            split_agu(2)
            split_agu(3)
            split_w(1, 1)
            for i in range(4):
                act.wait_ge(tm_done, i + 1)
                hb = slice((i // 2) * HT, (i // 2 + 1) * HT)
                nc.scalar.copy(t_hi[:, i % 2, hb], t_mask[:, i % 2, hb]).then_inc(th_done, 1)
            act.wait_ge(warm_used, 1)
            split_b(0, 0)
            split_b(0, 1)
            split_w(2, 0)
            make_silu(0, 0)
            make_silu(1, 1)
            split_w(3, 1)
            split_b(1, 0)
            split_b(1, 1)
            act.wait_ge(s_rates, 1)
            nc.scalar.activation(small("ea"), small("ar"), ACT.Exp).then_inc(s_exp1, 1)
            nc.scalar.activation(small("tnh"), small("ar"), ACT.Tanh, scale=0.5).then_inc(s_exp1, 1)
            act.wait_ge(s_ampin, 2)
            nc.scalar.activation(amp[:], amp[:], ACT.Exp).then_inc(s_amp, 1)
            nc.scalar.activation(amp_g[:], amp_g[:], ACT.Exp).then_inc(s_amp, 1)
            make_silu(2, 0)
            split_w(4, 0)
            nc.scalar.activation(small("sh"), small("r1"), ACT.Sin, scale=0.5).then_inc(s_exp1, 1)
            nc.scalar.activation(small("sn"), small("r1"), ACT.Sin).then_inc(s_exp1, 1)
            act.wait_ge(s_ang, 1)
            nc.scalar.activation(turn[:], ang[:], ACT.Sin).then_inc(s_sin, 1)
            split_w(5, 1)
            act.wait_ge(s_ang, 2)
            nc.scalar.activation(turn_g[:], ang_g[:], ACT.Sin).then_inc(s_sin, 1)
            split_b(2, 0)
            make_silu(3, 1)
            split_b(2, 1)
            make_silu(4, 0)
            with act.Fori(0, 2) as i:
                act.wait_ge(d_w[0], 16 * (i + 4))
                split_w(2 * i + 6, 0)
                split_b(i + 3, 0)
                make_silu(2 * i + 5, 1)
                act.wait_ge(d_w[1], 16 * (i + 4))
                split_w(2 * i + 7, 1)
                split_b(i + 3, 1)
                make_silu(2 * i + 6, 0)
            split_w(10, 0)
            split_b(5, 0)
            make_silu(9, 1)

            def split_wd(u, j, s):
                if isinstance(u, int) and u in (0, WD_FIRST):
                    act.wait_ge(d_wd[u // WD_FIRST], 16)
                if isinstance(u, int) and u < 2:
                    act.wait_ge(s_e, 2)
                else:
                    act.wait_ge(down_used, u - 1)
                nc.scalar.copy(wd_hi[s][:], wd_raw[:, bass.ds(j, 1), :].rearrange("p o c -> p (o c)")).then_inc(wdh_done, 1)

            def split_ad(j, s):
                if isinstance(j, int) and j < 2:
                    act.wait_ge(d_ad, 16 * NB)
                    act.wait_ge(bl_done, 8)
                    act.wait_ge(bh_done, 8)
                else:
                    act.wait_ge(down_used, j - 1)
                nc.scalar.copy(ad_hi[s][:].rearrange("p (b r) -> p b r", r=RANK),
                               ad_raw[:, :, bass.ds(j * RANK, RANK)]).then_inc(adh_done, 1)

            def split_ha(j, s):
                if isinstance(j, int) and j == 0:
                    act.wait_ge(w_used, 10)
                elif isinstance(j, int) and j == 1:
                    act.wait_ge(gu_done, FC)
                else:
                    act.wait_ge(down_used, j - 1)
                act.wait_ge(hid_done, j + 1)
                nc.scalar.copy(ha_hi[s][:], hid[:, :, bass.ds(j * HT, HT)]).then_inc(hh_done, 1)

            def split_a(j, s):
                split_ad(j, s)
                split_ha(j, s)
                split_wd(j, j, s)

            split_a(0, 0)
            make_silu(10, 0)
            split_a(1, 1)
            split_a(2, 0)
            act.wait_ge(d_bd, 16 * NG)
            for g in range(NG):
                nc.scalar.copy(bd_hi[:, g, :], bd_raw[:, g, :]).then_inc(bdh_done, 1)
                split_a(3 + g, (3 + g) % 2)
            with act.Fori(0, 2) as i:
                split_a(2 * i + 7, 1)
                split_a(2 * i + 8, 0)

            def split_b_unit(j, s):
                if isinstance(j, int) and j < 2:
                    act.wait_ge(w_used, FC)
                else:
                    act.wait_ge(down_used, j + 10)
                nc.scalar.copy(hb_hi[s][:], hid[:, 1, bass.ds(j * HT, HT)]).then_inc(hh_done, 1)

            split_b_unit(0, 0)
            split_wd(FC, 0, 1)
            act.wait_ge(tdm_done, 1)
            nc.scalar.copy(td_hi[:], td_mask[:]).then_inc(tdh_done, 1)
            split_b_unit(1, 1)
            split_wd(FC + 1, 1, 0)
            with act.Fori(0, 4) as i:
                split_b_unit(2 * i + 2, 0)
                split_wd(2 * i + FC + 2, 2 * i + 2, 1)
                split_b_unit(2 * i + 3, 1)
                split_wd(2 * i + FC + 3, 2 * i + 3, 0)
            split_b_unit(10, 0)
            split_wd(2 * FC - 1, FC - 1, 1)

            act.wait_ge(hl_done, 2 * FC)
            for t in range(2 * NQ):
                act.wait_ge(d_t[t % NQ], 16 * (t // NQ + 1))
                if t >= 2:
                    act.wait_ge(conv_done, t - 1)
                nc.scalar.copy(trev[t % 2][:].rearrange("p n (d q) -> p (n d) q", q=P),
                               toep[t % NQ][:].rearrange("p n (d q) -> p (n d) q", q=P)[:, :, ::-1],
                               ).then_inc(rev_done, 1)

        @block.vector
        def _(dve):
            v = nc.vector
            chain = [0]

            def link(ins):
                chain[0] += 1
                ins.then_inc(dve_chain, 1)
                dve.wait_ge(dve_chain, chain[0])

            def split_x(k):
                dve.wait_ge(xh_done, k + 1)
                v.tensor_tensor(x_lo[:, k, :], x_raw[:, k, :], x_hi[:, k, :].bitcast(F32),
                                ALU.subtract).then_inc(xl_done, 1)

            v.memset(zeros[:], 0.0).then_inc(zeros_ready, 1)
            v.memset(warm[:], 0.0).then_inc(warm_ready, 1)
            split_x(0)
            def split_w(j, s_):
                dve.wait_ge(wh_done, j + 1)
                v.tensor_tensor(w_lo[s_][:], w_raw[s_][:], w_hi[s_][:].bitcast(F32),
                                ALU.subtract).then_inc(wl_done, 1)

            split_w(0, 0)
            for k in range(1, KC):
                split_x(k)
            for g in range(NG):
                dve.wait_ge(aguh_done, g + 1)
                v.tensor_tensor(
                    agu_lo[g][:].rearrange("p c (b r) -> p c b r", r=RANK),
                    agu_raw[:, g * GB:(g + 1) * GB, :].rearrange("p b (c r) -> p c b r", r=RANK),
                    agu_hi[g][:].bitcast(F32).rearrange("p c (b r) -> p c b r", r=RANK),
                    ALU.subtract).then_inc(agul_done, 1)
            split_w(1, 1)

            dve.wait_ge(d_small, 64)
            link(v.tensor_scalar(rows_f[:], ints_sb[:, NB:NB + NG], float(RANK), c_col(C_RANK), ALU.mult, ALU.add))
            for part in range(NPART):
                link(v.tensor_scalar(rows[:, part, :], rows_f[:], float(part * NAD * RANK), None, ALU.add))
            v.tensor_copy(rows[:, NPART, :], rows_f[:]).then_inc(idx_ready, 1)
            block_mask = spread(cst[:, C_BLOCK:C_BLOCK + GB], [[0, HT // GB], [1, GB]])
            def mask_t(i):
                half, gu = i // 2, i % 2
                hb = slice(half * HT, (half + 1) * HT)
                dve.wait_ge(la_done, 2 * (half + 1))
                v.tensor_tensor(t_mask[:, gu, hb].rearrange("p (n b) -> p n b", b=GB),
                                banks[:, 4 + 2 * gu + half, :].rearrange("p (n b) -> p n b", b=GB),
                                block_mask, ALU.mult).then_inc(tm_done, 1)
                dve.wait_ge(th_done, i + 1)
                v.tensor_tensor(t_lo[:, gu, hb], t_mask[:, gu, hb], t_hi[:, gu, hb].bitcast(F32),
                                ALU.subtract).then_inc(tl_done, 1)

            mask_t(0)
            mask_t(1)
            mask_t(2)
            mask_t(3)

            def split_b(pair, s_):
                dve.wait_ge(bh_done, 2 * pair + s_ + 1)
                if not (isinstance(pair, int) and pair == 0):
                    dve.wait_ge(gu_done, 2 * pair + s_ - 1)
                v.tensor_tensor(b_lo[s_][:], b_raw[:, bass.ds(pair, 1), :, s_ * 2 * P:(s_ + 1) * 2 * P].rearrange(
                    "p o g c -> p (o g) c"), b_hi[s_][:].bitcast(F32), ALU.subtract).then_inc(bl_done, 1)

            split_b(0, 0)
            split_b(0, 1)

            def make_hid(j, s_):
                dve.wait_ge(silu_done, j + 1)
                v.tensor_tensor(hid[:, :, bass.ds(j * HT, HT)], silu[s_][:].rearrange("p (h t) -> p h t", h=2),
                                banks[:, 4 * s_ + 2:4 * s_ + 4, :], ALU.mult).then_inc(hid_done, 1)

            make_hid(0, 0)
            make_hid(1, 1)
            split_b(1, 0)
            split_b(1, 1)
            link(v.tensor_copy(lens_f[:], ints_sb[:, 0:NB]))
            link(v.tensor_tensor(mask[:], spread(lens_f[:], [[0, KC], [1, NB]]),
                                 spread(cst[:, C_POS:C_POS + KC], [[1, KC], [0, NB]]), ALU.is_gt))

            xx, kk, rr, pp, ee = (small(n, 2) for n in ("ldt", "k0", "r0", "p0", "e0"))
            link(v.tensor_scalar(kk, xx, LOG2E, ROUND, ALU.mult, ALU.add))
            link(v.tensor_scalar(kk, kk, ROUND, -126.0, ALU.subtract, ALU.max))
            link(v.tensor_scalar(kk, kk, 127.0, None, ALU.min))
            link(v.scalar_tensor_tensor(rr, kk, -LN2_HI, xx, ALU.mult, ALU.add))
            link(v.scalar_tensor_tensor(rr, kk, -LN2_LO, rr, ALU.mult, ALU.add))
            link(v.tensor_scalar(pp, rr, 1.0 / math.factorial(7), None, ALU.mult))
            for n in range(6, 0, -1):
                link(v.scalar_tensor_tensor(pp, pp, 1.0 / math.factorial(n), rr, ALU.add, ALU.mult))
            link(v.tensor_scalar(ee.bitcast(I32), kk, 127.0, 2.0 ** 23, ALU.add, ALU.mult))
            link(v.scalar_tensor_tensor(small("dt", 2), pp, 1.0, ee, ALU.add, ALU.mult))

            def reduce_turns(r, x, k, turns=None):
                if turns is None:
                    link(v.tensor_scalar(k, x, INV_2PI, ROUND, ALU.mult, ALU.add))
                    link(v.tensor_scalar(k, k, ROUND, None, ALU.subtract))
                else:
                    link(v.tensor_scalar(k, x, INV_2PI, turns, ALU.mult, ALU.add))
                    link(v.tensor_scalar(k, k, ROUND, ROUND, ALU.add, ALU.subtract))
                link(v.scalar_tensor_tensor(r, k, -PI2_1, x, ALU.mult, ALU.add))
                link(v.scalar_tensor_tensor(r, k, -PI2_2, r, ALU.mult, ALU.add))

            s = small
            link(v.scalar_tensor_tensor(s("ar"), s("are"), -1.0, s("dt"), ALU.mult, ALU.mult))
            link(v.tensor_tensor(s("th"), s("ai"), s("dt"), ALU.mult))
            link(v.tensor_scalar(s("ar32"), s("ar"), float(LJ), None, ALU.mult))
            reduce_turns(s("r1"), s("th"), s("hk"))
            link(v.tensor_scalar(s("ra"), s("r1"), float(LJ), None, ALU.mult))
            v.tensor_scalar(s("r1"), s("r1"), PI_IN, -PI_IN, ALU.min, ALU.max).then_inc(s_rates, 1)
            dve.wait_ge(s_rates, 1)
            reduce_turns(s("ra"), s("ra"), s("hk"))

            def phase(seg, col):
                link(v.tensor_scalar(seg, seg, c_col(col), PI_IN, ALU.add, ALU.min))

            link(v.tensor_tensor(ang[:].rearrange("p (h j) -> p h j", j=LJ), spread(s("r1"), [[1, NN], [0, LJ]]),
                                 spread(cst[:, C_J:C_J + LJ], [[0, NN], [1, LJ]]), ALU.mult))
            reduce_turns(ang[:], ang[:], turn[:], c_col(C_PHE))
            phase(ang[:], C_PHE + 1)
            v.tensor_scalar(ang[:], ang[:], -PI_IN, None, ALU.max).then_inc(s_ang, 1)

            make_hid(2, 0)
            g_len = NN * LA
            for part in range(2):
                link(v.tensor_tensor(ang_g[:, part * g_len:(part + 1) * g_len].rearrange("p (h a) -> p h a", a=LA),
                                     spread(s("ra"), [[1, NN], [0, LA]]),
                                     spread(cst[:, C_J:C_J + LA], [[0, NN], [1, LA]]), ALU.mult))
            for part, col in ((0, C_PHU), (1, C_PHV)):
                seg = slice(part * g_len, (part + 1) * g_len)
                reduce_turns(ang_g[:, seg], ang_g[:, seg], turn_g[:, seg], c_col(col))
                phase(ang_g[:, seg], col + 1)
            v.tensor_scalar(ang_g[:], ang_g[:], -PI_IN, None, ALU.max).then_inc(s_ang, 1)

            dve.wait_ge(s_exp1, 4)
            link(v.scalar_tensor_tensor(s("em"), s("ea"), 1.0, s("tnh"), ALU.add, ALU.mult))
            link(v.scalar_tensor_tensor(s("cm"), s("sh"), -2.0, s("sh"), ALU.mult, ALU.mult))
            link(v.tensor_tensor(s("zre"), s("ea"), s("cm"), ALU.mult))
            link(v.tensor_tensor(s("zre"), s("zre"), s("em"), ALU.add))
            link(v.tensor_tensor(s("zim"), s("ea"), s("sn"), ALU.mult))
            link(v.tensor_tensor(s("q1"), s("are"), s("are"), ALU.mult))
            link(v.tensor_tensor(s("den"), s("ai"), s("ai"), ALU.mult))
            link(v.tensor_tensor(s("den"), s("den"), s("q1"), ALU.add))
            link(v.reciprocal(s("rden"), s("den")))
            link(v.tensor_tensor(s("q1"), s("zim"), s("ai"), ALU.mult))
            link(v.tensor_tensor(s("q2"), s("zre"), s("are"), ALU.mult))
            link(v.tensor_tensor(s("q1"), s("q1"), s("q2"), ALU.subtract))
            link(v.tensor_tensor(s("q3"), s("zim"), s("are"), ALU.mult))
            link(v.tensor_tensor(s("q4"), s("zre"), s("ai"), ALU.mult))
            link(v.tensor_tensor(s("q3"), s("q3"), s("q4"), ALU.add))
            link(v.scalar_tensor_tensor(s("q1"), s("q1"), 2.0, s("rden"), ALU.mult, ALU.mult))
            link(v.scalar_tensor_tensor(s("q3"), s("q3"), -2.0, s("rden"), ALU.mult, ALU.mult))
            link(v.tensor_tensor(s("sre"), s("cr"), s("q1"), ALU.mult))
            link(v.tensor_tensor(s("q2"), s("ci"), s("q3"), ALU.mult))
            link(v.tensor_tensor(s("sre"), s("sre"), s("q2"), ALU.subtract))
            link(v.tensor_tensor(s("sim"), s("cr"), s("q3"), ALU.mult))
            link(v.tensor_tensor(s("q4"), s("ci"), s("q1"), ALU.mult))
            v.tensor_tensor(s("sim"), s("sim"), s("q4"), ALU.add).then_inc(s_cs, 1)

            split_b(2, 0)
            make_hid(3, 1)
            split_b(2, 1)
            make_hid(4, 0)
            dve.wait_ge(s_e, 2)
            with dve.Fori(0, 2) as i:
                split_b(i + 3, 0)
                make_hid(2 * i + 5, 1)
                split_b(i + 3, 1)
                make_hid(2 * i + 6, 0)
            split_b(5, 0)
            make_hid(9, 1)

            def split_ad(j, s_):
                dve.wait_ge(adh_done, j + 1)
                if not (isinstance(j, int) and j < 2):
                    dve.wait_ge(down_used, j - 1)
                v.tensor_tensor(ad_lo[s_][:].rearrange("p (b r) -> p b r", r=RANK), ad_raw[:, :, bass.ds(j * RANK, RANK)],
                                ad_hi[s_][:].bitcast(F32).rearrange("p (b r) -> p b r", r=RANK),
                                ALU.subtract).then_inc(adl_done, 1)

            def split_ha(j, s_):
                dve.wait_ge(hh_done, j + 1)
                v.tensor_tensor(ha_lo[s_][:], hid[:, :, bass.ds(j * HT, HT)], ha_hi[s_][:].bitcast(F32),
                                ALU.subtract).then_inc(hl_done, 1)

            def split_a(j, s_):
                split_ad(j, s_)
                split_ha(j, s_)

            split_a(0, 0)
            make_hid(10, 0)
            dve.wait_ge(k_mm, 1)
            link(v.tensor_copy(k_sb[:].rearrange("a h j -> a (h j)"),
                               banks[0:LA, 6:8, :].rearrange("p h t -> p (h t)")))
            v.tensor_tensor(k_sb[0:1, :, 0:1], k_sb[0:1, :, 0:1], skip_sb[:].rearrange("p (h o) -> p h o", o=1),
                            ALU.add).then_inc(k_ready, 1)
            with dve.Fori(0, 5) as i:
                split_a(2 * i + 1, 1)
                split_a(2 * i + 2, 0)

            def split_hb(j, s_):
                dve.wait_ge(hh_done, FC + j + 1)
                v.tensor_tensor(hb_lo[s_][:], hid[:, 1, bass.ds(j * HT, HT)], hb_hi[s_][:].bitcast(F32),
                                ALU.subtract).then_inc(hl_done, 1)

            def residual(half, c, bank):
                dve.wait_ge(y_done, half * KC + c + 1)
                ins = v.tensor_tensor(
                    x1[:, :, c, half * 2 * GB:(half + 1) * 2 * GB].rearrange("p n (g b) -> p g n b", b=GB),
                    banks[:, bank, :].rearrange("p (g n b) -> p g n b", n=NN, b=GB),
                    x_res[:, c, half * HT:(half + 1) * HT].rearrange("p (g n b) -> p g n b", n=NN, b=GB), ALU.add)
                ins.then_inc(x1_done if half else bank_free, 1)

            split_hb(0, 0)
            dve.wait_ge(td_done, 1)
            v.tensor_tensor(td_mask[:].rearrange("p (n b) -> p n b", b=GB),
                            banks[:, 4:6, :].rearrange("p h (n b) -> p (h n) b", b=GB),
                            spread(cst[:, C_BLOCK:C_BLOCK + GB], [[0, TOK // GB], [1, GB]]),
                            ALU.mult).then_inc(tdm_done, 1)
            split_hb(1, 1)
            dve.wait_ge(tdh_done, 1)
            v.tensor_tensor(td_lo[:], td_mask[:], td_hi[:].bitcast(F32), ALU.subtract).then_inc(tdl_done, 1)
            dve.wait_ge(d_xres, 16)
            for c in range(KC):
                split_hb(2 + c, c % 2)
                residual(0, c, c)
            split_hb(6, 0)
            with dve.Fori(0, 2) as i:
                split_hb(2 * i + 7, 1)
                split_hb(2 * i + 8, 0)
            for c in range(KC):
                residual(1, c, 4 + c)

            with dve.Fori(0, 2) as it:
                for q in range(NQ):
                    dve.wait_ge(conv_done, NQ * it + q + 1)
                    n0 = bass.ds(NQ * QN * it + QN * q, QN)
                    tmp = conv_tmp[q % 2]
                    v.tensor_tensor(tmp[:], banks[:, q, :].rearrange("p (n c) -> p n c", n=QN),
                                    spread(mask[:], [[0, QN], [1, KC * NB]]), ALU.mult).then_inc(bank_free, 1)
                    dve.wait_ge(bank_free, KC + NQ * it + q + 1)
                    x1n = x1[:, n0, :, :].rearrange("p n c b -> p n (c b)")
                    v.tensor_tensor(x1n, x1n, tmp[:], ALU.add).then_inc(out_ready, 1)

        @block.tensor
        def _(pe):
            mm = nc.tensor.matmul

            def three(dst, st_hi, st_lo, mv_hi, mv_lo, start, stop):
                mm(dst, st_hi, mv_hi, start=start, stop=False)
                mm(dst, st_hi, mv_lo, start=False, stop=False)
                return mm(dst, st_lo, mv_hi, start=False, stop=stop)

            def dense(s, half, gu):
                for k in range(KC):
                    c = gu * KC + k
                    hb = slice(half * HT, (half + 1) * HT)
                    last = three(banks[:, 4 * s + 2 * gu + half, :], w_hi[s][:, c, :], w_lo[s][:, c, :],
                                 x_hi[:, k, hb], x_lo[:, k, hb], k == 0, False)
                return last

            def lora(s):
                for half in range(2):
                    for gu in range(2):
                        for gg in range(2):
                            g = 2 * half + gg
                            last = three(banks[:, 4 * s + 2 * gu + half, gg * GT:(gg + 1) * GT],
                                         b_hi[s][:, g, gu * P:(gu + 1) * P], b_lo[s][:, g, gu * P:(gu + 1) * P],
                                         t_hi[:, gu, g * GT:(g + 1) * GT], t_lo[:, gu, g * GT:(g + 1) * GT],
                                         False, gg == 1)
                last.then_inc(gu_done, 1)

            pe.wait_ge(warm_ready, 1)
            for _ in range(WARM):
                last = mm(banks[:, 7, :], warm[:, 0:P], warm[:], start=True, stop=True)
            last.then_inc(warm_used, 1)
            pe.wait_ge(wh_done, 1)
            pe.wait_ge(wl_done, 1)
            for k in range(KC):
                pe.wait_ge(xh_done, k + 1)
                pe.wait_ge(xl_done, k + 1)
                for half in range(2):
                    for gu in range(2):
                        c = gu * KC + k
                        hb = slice(half * HT, (half + 1) * HT)
                        last = three(banks[:, 2 * gu + half, :], w_hi[0][:, c, :], w_lo[0][:, c, :],
                                     x_hi[:, k, hb], x_lo[:, k, hb], k == 0, False)
            last.then_inc(w_used, 1)
            for g in range(NG):
                pe.wait_ge(aguh_done, g + 1)
                pe.wait_ge(agul_done, g + 1)
                for gu in range(2):
                    for k in range(KC):
                        c = gu * KC + k
                        last = three(banks[:, 4 + 2 * gu + g // 2, (g % 2) * GT:(g % 2 + 1) * GT],
                                     agu_hi[g][:, c, :], agu_lo[g][:, c, :], x_hi[:, k, g * GT:(g + 1) * GT],
                                     x_lo[:, k, g * GT:(g + 1) * GT], k == 0, k == KC - 1)
                last.then_inc(la_done, 1)
            pe.wait_ge(wh_done, 2)
            pe.wait_ge(wl_done, 2)
            for half in range(2):
                for gu in range(2):
                    pe.wait_ge(tm_done, 2 * half + gu + 1)
                    last = dense(1, half, gu)
            last.then_inc(w_used, 1)
            pe.wait_ge(th_done, 4)
            pe.wait_ge(tl_done, 4)
            for s in range(2):
                pe.wait_ge(bh_done, s + 1)
                pe.wait_ge(bl_done, s + 1)
                lora(s)

            def chunk(j, s):
                pe.wait_ge(wh_done, j + 1)
                pe.wait_ge(wl_done, j + 1)
                pe.wait_ge(hid_done, j - 1)
                for half in range(2):
                    for gu in range(2):
                        last = dense(s, half, gu)
                last.then_inc(w_used, 1)
                pe.wait_ge(bh_done, j + 1)
                pe.wait_ge(bl_done, j + 1)
                lora(s)

            with pe.Fori(0, 4) as i:
                chunk(2 * i + 2, 0)
                chunk(2 * i + 3, 1)
            chunk(10, 0)

            pe.wait_ge(s_e, 2)
            pe.wait_ge(hid_done, 10)
            for h in range(NN):
                col = (h % (NN // 2)) * LJ
                last = mm(banks[0:LA, 6 + h // (NN // 2), col:col + LJ], ssm_g[:, h, :], ssm_e[:, h, :],
                          start=True, stop=True)
            last.then_inc(k_mm, 1)

            def down(s, half_bank, order, mv_hi, mv_lo, s_w, start, waits=()):
                for n, c in enumerate(order):
                    if n < len(waits) and waits[n] is not None:
                        pe.wait_ge(*waits[n])
                    last = three(banks[:, half_bank + c, :], wd_hi[s_w][:, c * P:(c + 1) * P],
                                 wd_lo[s_w][:, c * P:(c + 1) * P], mv_hi, mv_lo, start, False)
                last.then_inc(down_used, 1)

            def unit_a(j, s, first=False, final=False):
                pe.wait_ge(adh_done, j + 1)
                pe.wait_ge(adl_done, j + 1)
                pe.wait_ge(hh_done, j + 1)
                pe.wait_ge(hl_done, j + 1)
                for g in range(NG):
                    half, gg = g // 2, g % 2
                    cols = slice(gg * GT, (gg + 1) * GT)
                    last = three(banks[:, 4 + half, cols], ad_hi[s][:, g * P:(g + 1) * P],
                                 ad_lo[s][:, g * P:(g + 1) * P], ha_hi[s][:, half, cols], ha_lo[s][:, half, cols],
                                 first and gg == 0, final and gg == 1)
                if final:
                    last.then_inc(td_done, 1)
                pe.wait_ge(wdh_done, j + 1)
                pe.wait_ge(wdl_done, j + 1)
                if first:
                    pe.wait_ge(hid_done, FC)
                down(s, 0, range(KC), ha_hi[s][:, 0, :], ha_lo[s][:, 0, :], s, first)

            unit_a(0, 0, first=True)
            with pe.Fori(0, 4) as i:
                unit_a(2 * i + 1, 1)
                unit_a(2 * i + 2, 0)
            unit_a(9, 1)
            unit_a(10, 0, final=True)

            def unit_b(j, s, first=False):
                pe.wait_ge(hh_done, FC + j + 1)
                pe.wait_ge(hl_done, FC + j + 1)
                pe.wait_ge(wdh_done, FC + j + 1)
                pe.wait_ge(wdl_done, FC + j + 1)
                waits = ((k_ready, 1), None, (tdm_done, 1)) if first else ()
                down(s, 4, (2, 3, 0, 1), hb_hi[s][:], hb_lo[s][:], 1 - s, first, waits)

            def lora_down(half):
                for c in range(KC):
                    for gg in range(2):
                        g = 2 * half + gg
                        if half == 0 and c == 0:
                            pe.wait_ge(bdh_done, NG)
                            pe.wait_ge(bdl_done, NG)
                        last = three(banks[:, 4 * half + c, gg * GT:(gg + 1) * GT], bd_hi[:, g, c * P:(c + 1) * P],
                                     bd_lo[:, g, c * P:(c + 1) * P], td_hi[:, g * GT:(g + 1) * GT],
                                     td_lo[:, g * GT:(g + 1) * GT], False, gg == 1)
                    last.then_inc(y_done, 1)

            unit_b(0, 0, first=True)
            pe.wait_ge(tdh_done, 1)
            pe.wait_ge(tdl_done, 1)
            lora_down(0)
            with pe.Fori(0, 5) as i:
                unit_b(2 * i + 1, 1)
                unit_b(2 * i + 2, 0)
            lora_down(1)

            pe.wait_ge(x1_done, KC)
            with pe.Fori(0, 2) as it:
                for q in range(NQ):
                    pe.wait_ge(rev_done, NQ * it + q + 1)
                    pe.wait_ge(bank_free, NQ * it + q + 1)
                    for n in range(QN):
                        src = x1[:, bass.ds(NQ * QN * it + QN * q + n, 1), :, :].rearrange("p n c b -> p (n c b)")
                        for d in range(KC):
                            last = mm(banks[:, q, n * P + d * NB:(n + 1) * P], trev[q % 2][:, n, d * P:(d + 1) * P],
                                      src[:, 0:(KC - d) * NB], start=(d == 0), stop=(d == KC - 1))
                    last.then_inc(conv_done, 1)


def kernel(x, itok_B_2_6, itok_B_8_3872, L0_cond_W_gate, L0_cond_W_up, L0_cond_W_down, L0_cond_A_gate,
           L0_cond_B_gate, L0_cond_A_up, L0_cond_B_up, L0_cond_A_down, L0_cond_B_down, L1_cond_log_dt,
           L1_cond_C, L1_cond_log_A_real, L1_cond_A_imag, L1_cond_D):
    import concourse.bacc as bacc
    from concourse.bass_utils import run_bass_kernel_spmd

    def pad_f(a, axis, size=FC * P):
        width = [(0, 0)] * a.ndim
        width[axis] = (0, size - a.shape[axis])
        return np.pad(a, width)

    x = np.asarray(x)
    x_t = x.reshape(NG, GB, NN, KC, P).transpose(4, 3, 0, 2, 1).reshape(P, KC, TOK)
    w = np.stack([pad_f(np.asarray(a), 0) for a in (L0_cond_W_gate, L0_cond_W_up)])
    w_gu = w.reshape(2, FC, P, KC, P).transpose(1, 4, 0, 3, 2).reshape(FC, P, 2 * KC, P)
    w_d = pad_f(np.asarray(L0_cond_W_down), 1).T.reshape(FC, P, KC, P)[..., ::-1].transpose(1, 0, 2, 3)
    w_d = w_d.reshape(P, FC, H)
    a = np.stack([np.asarray(L0_cond_A_gate)[0], np.asarray(L0_cond_A_up)[0]])
    a_gu = a.reshape(2, NAD, RANK, KC, P).transpose(1, 4, 0, 3, 2).reshape(NAD, P, 2 * KC * RANK)
    a_d = pad_f(np.asarray(L0_cond_A_down)[0], 2).reshape(NAD, RANK, FC, P).transpose(0, 3, 2, 1)
    a_d = a_d.reshape(NAD, P, FC * RANK)
    b = np.stack([pad_f(np.asarray(m)[0], 1, 2 * NPART * P) for m in (L0_cond_B_gate, L0_cond_B_up)])
    b_gu = b.reshape(2, NAD, NPART, 2, P, RANK).transpose(2, 1, 5, 3, 0, 4).reshape(NPART * NAD * RANK, 4 * P)
    b_d = np.asarray(L0_cond_B_down)[0].transpose(0, 2, 1).reshape(NAD * RANK, KC, P)[..., ::-1]
    b_d = b_d.reshape(NAD * RANK, H)
    idx = np.asarray(itok_B_2_6)
    ints = np.concatenate([np.tile(np.asarray(itok_B_8_3872), (P, 1)),
                           np.repeat(idx.reshape(NG, GB).T, RANK, axis=0)], axis=1)
    c = np.asarray(L1_cond_C)
    rates = np.stack([np.tile(np.asarray(L1_cond_log_dt), (MODES, 1)), np.asarray(L1_cond_log_A_real).T,
                      np.asarray(L1_cond_A_imag).T, c[:, :, 0].T, c[:, :, 1].T], axis=1)
    params = np.concatenate([rates, rates], axis=0).reshape(P, 5 * NN)
    skip = np.asarray(L1_cond_D).reshape(1, NN)

    nc = bacc.Bacc("TRN2", target_bir_lowering=False, num_devices=1)
    arrays, args = {}, []
    for name, v in (("x_t", x_t), ("x_rev", x_t[::-1]), ("w_gu", w_gu), ("w_d", w_d), ("a_gu", a_gu), ("a_d", a_d), ("b_gu", b_gu),
                    ("b_d", b_d), ("idx_row", idx.reshape(1, NB)), ("ints", ints), ("params", params),
                    ("skip", skip), ("consts", constants())):
        v = np.ascontiguousarray(v)
        arrays[name] = v
        args.append(nc.dram_tensor(name, v.shape, mybir.dt.from_np(v.dtype), kind="ExternalInput").ap())
    out = nc.dram_tensor("out", (P, NN, KC * NB), F32, kind="ExternalOutput").ap()
    program(nc, *args, out)
    r = run_bass_kernel_spmd(nc, [arrays], core_ids=[0])
    y = r.results[0]["out"][::-1]
    return y.reshape(P, NN, KC, NB).transpose(3, 1, 2, 0).reshape(NB, NN, H)
```

```python
import math
from contextlib import ExitStack

import numpy as np

import concourse.bass as bass
from concourse import mybir
from concourse.alu_op_type import AluOpType as ALU

F32 = mybir.dt.float32
F32R = mybir.dt.float32r
I32 = mybir.dt.int32
ACT = mybir.ActivationFunctionType

P = 128
NB, NN, H, F = 32, 32, 512, 1376
WARM = 3
WD_FIRST = 3
RANK, NAD = 16, 16
LORA_SCALE = 0.5
FC = -(-F // P)
KC = H // P
GB = P // RANK
NG = NB // GB
GT = GB * NN
TOK = NB * NN
HT = TOK // 2
NPART = (FC + 1) // 2
MODES = 64
PB = 2
LA, LJ = 16, 32
PAD = P
QN = 4
NQ = 4
STEPS = NN // QN
SBUF0 = 16512

C_J, C_PHE, C_PHU, C_PHV, C_RANK, C_BLOCK, C_POS = 0, 32, 34, 36, 38, 39, 47
NCONST = C_POS + KC

LOG2E = 1.0 / math.log(2.0)
LN2_HI, LN2_LO = 0.693145751953125, 1.42860676533018518e-06
INV_2PI = 1.0 / (2.0 * math.pi)
PI2_1 = 6.28125
PI2_2 = 2.0 * math.pi - PI2_1
PI_IN = 3.1415925
ROUND = 1.5 * 2.0 ** 23


def constants():
    c = np.zeros((P, NCONST), np.float32)
    p = np.arange(P)
    imag = p // MODES
    c[:, C_J:C_J + LJ] = np.arange(LJ)
    for col, turns in ((C_PHE, (0.25, 0.0)), (C_PHU, (0.25, 0.5)), (C_PHV, (0.0, 0.25))):
        c[:, col] = np.array(turns)[imag]
        c[:, col + 1] = np.array(turns)[imag] * 2.0 * math.pi
    c[:, C_RANK] = p % RANK
    c[:, C_BLOCK:C_BLOCK + GB] = LORA_SCALE * (p[:, None] // RANK == np.arange(GB))
    c[:, C_POS:C_POS + KC] = (P - 1 - p[:, None]) + P * np.arange(KC)
    return c


def program(nc, x_t, x_rev, w_gu, w_d, a_gu, a_d, b_gu, b_d, idx_row, ints, params, skip, eye, consts, out):
    ctx = ExitStack()
    with ctx:
        def sem(name):
            return ctx.enter_context(nc.semaphore(name))

        def at(name, kib, shape, dt=F32):
            return nc.alloc_sbuf_tensor_at(name, shape, dt, offset=SBUF0 + int(kib * 1024))

        ctx.enter_context(nc.sbuf_tensor("slab", [P, (207 * 1024) // 4], F32))

        b_raw = at("b_raw", 0, [P, NPART, NG, 2 * 2 * P])
        x_raw = at("x_raw", 16, [P, KC, TOK])
        agu_raw = at("agu_raw", 32, [P, NB, RANK, 2 * KC])
        ad_raw = at("ad_raw", 0, [P, NB, FC * RANK])
        ad_rows = [at(f"ad_rows{s}", 24 + 4 * s, [P, NB * RANK]) for s in range(2)]
        toep = [at(f"toep{q}", 8 * q, [P, QN, H]) for q in range(NQ)]
        b_hi = [at(f"b_hi{s}", 56 - 8 * s, [P, NG, 2 * P], F32R) for s in range(2)]
        b_lo = [at(f"b_lo{s}", 60 - 8 * s, [P, NG, 2 * P], F32R) for s in range(2)]
        w_hi = [at(f"w_hi{s}", 64 + 8 * s, [P, 2 * KC, P], F32R) for s in range(2)]
        w_lo = [at(f"w_lo{s}", 68 + 8 * s, [P, 2 * KC, P], F32R) for s in range(2)]
        w_raw = [at(f"w_raw{s}", 80 + 4 * s, [P, 2 * KC, P]) for s in range(2)]
        ha_hi = [at("ha_hi0", 72, [P, HT], F32R), at("ha_hi1", 56, [P, HT], F32R)]
        ha_lo = [at("ha_lo0", 76, [P, HT], F32R), at("ha_lo1", 60, [P, HT], F32R)]
        hs = [at(f"hs{s}", 80 + 4 * s, [P, 2, HT]) for s in range(2)]
        hb_hi = [at(f"hb_hi{s}", 64 + 4 * s, [P, HT], F32R) for s in range(2)]
        hb_lo = [at(f"hb_lo{s}", 66 + 4 * s, [P, HT], F32R) for s in range(2)]
        wd_raw = at("wd_raw", 32, [P, FC, H])
        conv_tmp = [at(f"conv_tmp{s}", 80 + 2 * s, [P, QN, KC, NB]) for s in range(2)]
        conv_sb = [at(f"conv_sb{s}", 84 + 2 * s, [P, H]) for s in range(2)]
        t_mask = at("t_mask", 88, [P, 2, TOK])
        silu = [at(f"silu{s}", 88 + 4 * s, [P, TOK]) for s in range(2)]
        td_mask = at("td_mask", 88, [P, TOK])
        k_sb = at("k_sb", 92, [P, NN // 4, LA])
        ssm_e = at("ssm_e", 96, [P, NN, LJ])
        ssm_g = at("ssm_g", 100, [P, NN, LA])
        hid = at("hid", 102, [P, 2, FC * HT])
        ang = at("ang", 134, [P, NN * LJ])
        turn = at("turn", 138, [P, NN * LJ])
        amp = at("amp", 142, [P, NN * LJ])
        x1 = at("x1", 102, [P, NN, KC, NB])
        x_hi = at("x_hi", 146, [P, KC, TOK], F32R)
        x_lo = at("x_lo", 162, [P, KC, TOK], F32R)
        td_hi = at("td_hi", 146, [P, TOK], F32R)
        td_lo = at("td_lo", 150, [P, TOK], F32R)
        bd_raw = at("bd_raw", 154, [P, NG, H])
        bd_hi = at("bd_hi", 162, [P, NG, H], F32R)
        bd_lo = at("bd_lo", 170, [P, NG, H], F32R)
        t_hi = at("t_hi", 178, [P, 2, TOK], F32R)
        t_lo = at("t_lo", 186, [P, 2, TOK], F32R)
        x_res = at("x_res", 178, [P, KC, TOK])
        sm = at("sm", 194, [P, 40, NN])
        wd_hi = [at(f"wd_hi{s}", 194 + 4 * s, [P, H], F32R) for s in range(2)]
        wd_lo = [at(f"wd_lo{s}", 196 + 4 * s, [P, H], F32R) for s in range(2)]
        cst = at("cst", 202, [P, NCONST])
        ints_sb = at("ints_sb", 202.25, [P, NB + NG], I32)
        idx_sb = at("idx_sb", 202.5, [1, NB], I32)
        rows_f = at("rows_f", 203, [P, NG])
        rows = at("rows", 203.125, [P, NPART + 1, NG], I32)
        mask = at("mask", 203.25, [P, KC, NB])
        lens_f = at("lens_f", 203.75, [P, NB])
        zeros = at("zeros", 204, [NN, PAD])
        junk = at("junk", 204.5, [NN, 1])
        block_sb = at("block_sb", 205, [P, GB // PB, NN, PB])
        skip_sb = at("skip_sb", 206, [P, NN // 4, LA])
        eye_sb = at("eye_sb", 206.5, [P, P])
        ang_g = at("ang_g", 114, [P, 2 * NN * LA])
        turn_g = at("turn_g", 118, [P, 2 * NN * LA])
        warm = at("warm", 56, [P, HT])
        amp_g = at("amp_g", 199, [P, NN * LA])

        banks = ctx.enter_context(nc.psum_tensor("banks", [P, 8, HT], F32))

        k_pad = nc.dram_tensor("k_pad", (NN, PAD + H), F32, kind="Internal").ap()

        d_ints = sem("d_ints")
        d_small = sem("d_small")
        d_idx = sem("d_idx")
        d_first = sem("d_first")
        d_x_first = sem("d_x_first")
        d_x = [sem(f"d_x{k}") for k in range(KC)]
        d_w = [sem(f"d_w{s}") for s in range(2)]
        d_agu = [sem(f"d_agu{g}") for g in range(NG)]
        d_agu_pool = sem("d_agu_pool")
        d_b = sem("d_b")
        d_ad = sem("d_ad")
        d_bd = sem("d_bd")
        d_wd = [sem(f"d_wd{s}") for s in range(2)]
        d_xres = sem("d_xres")
        d_kpad = sem("d_kpad")
        d_t = [sem(f"d_t{q}") for q in range(NQ)]
        d_out = sem("d_out")
        idx_ready = sem("idx_ready")
        zeros_ready = sem("zeros_ready")
        block_ready = sem("block_ready")
        warm_ready = sem("warm_ready")
        warm_used = sem("warm_used")
        first_hi = sem("first_hi")
        first_lo = sem("first_lo")
        xh_done = sem("xh_done")
        xl_done = sem("xl_done")
        la_done = sem("la_done")
        tm_done = sem("tm_done")
        th_done = sem("th_done")
        tl_done = sem("tl_done")
        wh_done = sem("wh_done")
        wl_done = sem("wl_done")
        bh_done = sem("bh_done")
        bl_done = sem("bl_done")
        w_used = sem("w_used")
        gu_done = sem("gu_done")
        silu_done = sem("silu_done")
        hid_done = sem("hid_done")
        hh_done = sem("hh_done")
        hl_done = sem("hl_done")
        wdh_done = sem("wdh_done")
        wdl_done = sem("wdl_done")
        ad_done = sem("ad_done")
        hs_done = sem("hs_done")
        down_used = sem("down_used")
        td_done = sem("td_done")
        tdm_done = sem("tdm_done")
        tdh_done = sem("tdh_done")
        tdl_done = sem("tdl_done")
        bdh_done = sem("bdh_done")
        bdl_done = sem("bdl_done")
        y_done = sem("y_done")
        x1_done = sem("x1_done")
        bank_free = sem("bank_free")
        conv_done = sem("conv_done")
        sum_copied = sem("sum_copied")
        back_done = sem("back_done")
        out_ready = sem("out_ready")
        k_mm = sem("k_mm")
        k_ready = sem("k_ready")
        dve_chain = sem("dve_chain")
        pool_chain = sem("pool_chain")
        s_rates = sem("s_rates")
        s_exp1 = sem("s_exp1")
        s_cs = sem("s_cs")
        s_ampin = sem("s_ampin")
        s_amp = sem("s_amp")
        s_ang = sem("s_ang")
        s_sin = sem("s_sin")
        s_e = sem("s_e")

        block = ctx.enter_context(nc.Block())

        def by_k(w, k0, k1):
            return w[:].rearrange("p (g k) f -> p g k f", k=KC)[:, :, k0:k1, :]

        def spread(ap, dims):
            return bass.AP(tensor=ap.tensor, offset=ap.offset, ap=[list(ap.ap[0])] + dims)

        names = ("are dt x_ k_ r_ p_ s_ ai cr ci ar th r1 ra ea tnh sh sn em cm zre zim den rden "
                 "q1 q2 q3 q4 sre sim ars hk ldt lar").split()
        slot = {}
        for i, n_ in enumerate(["ldt", "lar", "ai", "cr", "ci", "k0", "k1", "r0", "r_1", "p0", "p1", "e0", "e1",
                                "dt", "are"] + [n for n in names if n not in ("ldt", "lar", "ai", "cr", "ci", "dt",
                                                                            "are", "x_", "k_", "r_", "p_", "s_")]):
            slot[n_] = i

        def small(name, width=1):
            return sm[:, slot[name]:slot[name] + width, :].rearrange("p a b -> p (a b)")

        def c_col(i):
            return cst[:, i:i + 1]

        @block.sync
        def _(sp):
            def load_toeplitz(q, turn_):
                first = k_pad[0:1, 0:1]
                src = bass.AP(tensor=first.tensor, offset=(turn_ * NQ + q) * QN * (PAD + H) + PAD - (P - 1),
                              ap=[[1, P], [PAD + H, QN], [1, H]])
                sp.dma_start(toep[q][:], src).then_inc(d_t[q], 16)

            sp.dma_start(by_k(w_raw[0], 0, 1), by_k(w_gu[0], 0, 1)).then_inc(d_first, 16)
            sp.dma_start(x_raw[:, 0, 0:HT], x_t[:, 0, 0:HT]).then_inc(d_x_first, 16)
            sp.dma_start(x_raw[:, 0, HT:TOK], x_t[:, 0, HT:TOK]).then_inc(d_x[0], 16)
            sp.dma_start(idx_sb[:], idx_row).then_inc(d_idx, 16)
            sp.dma_start(by_k(w_raw[0], 1, KC), by_k(w_gu[0], 1, KC)).then_inc(d_w[0], 16)
            for k in range(1, KC):
                sp.dma_start(x_raw[:, k, :], x_t[:, k, :]).then_inc(d_x[k], 16)
            sp.wait_ge(d_idx, 16)
            def gather_a(batches):
                _, ads = nc.values_load_multi_w_load_instructions(
                    idx_sb[0:1, batches], engines=[mybir.EngineType.SP], min_val=0, max_val=NAD - 1,
                    skip_runtime_bounds_check_because="an adaptor's index")
                for b, ad in zip(range(batches.start, batches.stop), ads):
                    sp.dma_start(agu_raw[:, b:b + 1, :, :].rearrange("p b r c -> p b (r c)"),
                                 a_gu[bass.ds(ad, 1), :, :].rearrange("o p c -> p o c")).then_inc(d_agu[b // GB], 16)

            gather_a(slice(0, GB))
            sp.dma_start(ints_sb[:], ints).then_inc(d_ints, 16)
            sp.dma_start(cst[:], consts).then_inc(d_ints, 16)
            sp.dma_start(w_raw[1][:], w_gu[1]).then_inc(d_w[1], 16)
            gather_a(slice(2 * GB, 3 * GB))
            sp.dma_start(sm[:, 0:5, :].rearrange("p a b -> p (a b)"), params).then_inc(d_small, 16)
            sp.dma_start(skip_sb[:], skip).then_inc(d_small, 16)
            sp.dma_start(eye_sb[:], eye).then_inc(d_small, 16)
            gather_a(slice(NB - GB // 2, NB))

            def load_w(j, s):
                sp.wait_ge(wh_done, j - 1)
                sp.wait_ge(wl_done, j - 1)
                sp.dma_start(w_raw[s][:], w_gu[bass.ds(j, 1)].rearrange("o p c f -> p (o c) f")).then_inc(d_w[s], 16)

            with sp.Fori(0, 3) as i:
                load_w(2 * i + 2, 0)
                load_w(2 * i + 3, 1)
            load_w(8, 0)
            sp.wait_ge(bh_done, 6)
            sp.wait_ge(bl_done, 6)
            with sp.Fori(0, NG) as g:
                _, ads = nc.values_load_multi_w_load_instructions(
                    idx_sb[0:1, bass.ds(g * GB, GB)], engines=[mybir.EngineType.SP], min_val=0, max_val=NAD - 1,
                    skip_runtime_bounds_check_because="an adaptor's index")
                for i, ad in enumerate(ads):
                    sp.dma_start(ad_raw[:, bass.ds(g * GB + i, 1), :],
                                 a_d[bass.ds(ad, 1), :, :].rearrange("o p c -> p o c")).then_inc(d_ad, 16)
            load_w(9, 1)
            load_w(10, 0)

            sp.wait_ge(bh_done, FC)
            sp.wait_ge(bl_done, FC)
            sp.wait_ge(gu_done, FC - 1)
            sp.dma_start(wd_raw[:, 0:WD_FIRST, :], w_d[:, 0:WD_FIRST, :]).then_inc(d_wd[0], 16)
            sp.dma_start(wd_raw[:, WD_FIRST:FC, :], w_d[:, WD_FIRST:FC, :]).then_inc(d_wd[1], 16)
            sp.wait_ge(gu_done, FC)
            sp.dma_start(x_res[:], x_rev).then_inc(d_xres, 16)
            sp.wait_ge(zeros_ready, 1)
            sp.dma_start(k_pad[:, 0:PAD], zeros[:]).then_inc(d_kpad, 16)
            sp.wait_ge(k_ready, 1)
            for t in range(4):
                sp.dma_start(k_pad[t * 8:(t + 1) * 8, PAD:PAD + H].rearrange("h (j a) -> j h a", a=LA),
                             k_sb[t * LJ:(t + 1) * LJ]).then_inc(d_kpad, 16)
            sp.wait_ge(d_kpad, 16 * 5)
            sp.wait_ge(down_used, FC)
            for q in range(NQ):
                load_toeplitz(q, 0)
            for q in range(NQ):
                sp.wait_ge(conv_done, q + 1)
                load_toeplitz(q, 1)
            for t in range(STEPS):
                sp.wait_ge(out_ready, t + 1 if t < STEPS - 1 else STEPS + 1)
                sp.dma_start(out[:, t * QN:(t + 1) * QN, :, :], x1[:, t * QN:(t + 1) * QN, :, :]).then_inc(d_out, 16)
            sp.wait_ge(d_out, 16 * STEPS)

        @block.gpsimd
        def _(pool):
            chain = [0]

            def link(ins):
                chain[0] += 1
                ins.then_inc(pool_chain, 1)
                pool.wait_ge(pool_chain, chain[0])

            def gather_part(part):
                for g in range(NG):
                    nc.gpsimd.indirect_dma_start(
                        out=b_raw[:, part, g, :], out_offset=None, in_=b_gu,
                        in_offset=bass.IndirectOffsetOnAxis(ap=rows[:, part, g:g + 1], axis=0)).then_inc(d_b, 16)

            def split_w(j, s):
                pool.wait_ge(wh_done, j + 1)
                if not (isinstance(j, int) and j < 2):
                    pool.wait_ge(w_used, j - 1)
                nc.gpsimd.tensor_tensor(w_lo[s][:], w_raw[s][:], w_hi[s][:].bitcast(F32),
                                        ALU.subtract).then_inc(wl_done, 1)

            pool.wait_ge(d_idx, 16)
            for batches in (slice(GB, 2 * GB), slice(NB - GB, NB - GB // 2)):
                _, ads = nc.values_load_multi_w_load_instructions(
                    idx_sb[0:1, batches], engines=[mybir.EngineType.Pool], min_val=0, max_val=NAD - 1,
                    skip_runtime_bounds_check_because="an adaptor's index")
                for b, ad in zip(range(batches.start, batches.stop), ads):
                    nc.gpsimd.dma_start(agu_raw[:, b:b + 1, :, :].rearrange("p b r c -> p b (r c)"),
                                        a_gu[bass.ds(ad, 1), :, :].rearrange("o p c -> p o c")
                                        ).then_inc(d_agu[1] if b < 2 * GB else d_agu_pool, 16)
            pool.wait_ge(idx_ready, 1)
            pool.wait_ge(d_agu[NG - 1], 8 * GB)
            gather_part(0)
            pool.wait_ge(d_b, 64)
            gather_part(1)
            pool.wait_ge(d_b, 128)
            pool.wait_ge(la_done, NG)
            pool.wait_ge(xh_done, KC)
            pool.wait_ge(xl_done, KC)
            pool.wait_ge(wl_done, 2)
            split_w(2, 0)
            gather_part(2)
            split_w(3, 1)
            pool.wait_ge(d_b, 64 * 3)
            gather_part(3)
            pool.wait_ge(s_rates, 1)
            nc.gpsimd.tensor_tensor(
                amp[:].rearrange("p (h j) -> p h j", j=LJ), spread(small("ars"), [[1, NN], [0, LJ]]),
                spread(cst[:, C_J:C_J + LJ], [[0, NN], [1, LJ]]), ALU.mult).then_inc(s_ampin, 1)
            nc.gpsimd.tensor_tensor(
                amp_g[:].rearrange("p (h a) -> p h a", a=LA), spread(small("ar"), [[1, NN], [0, LA]]),
                spread(cst[:, C_J:C_J + LA], [[0, NN], [1, LA]]), ALU.mult).then_inc(s_ampin, 1)
            split_w(4, 0)
            pool.wait_ge(s_amp, 1)
            pool.wait_ge(s_sin, 1)
            nc.gpsimd.tensor_tensor(ssm_e[:].rearrange("p h j -> p (h j)"), turn[:], amp[:],
                                    ALU.mult).then_inc(s_e, 1)
            split_w(5, 1)
            pool.wait_ge(s_amp, 2)
            pool.wait_ge(s_sin, 2)
            pool.wait_ge(s_cs, 1)
            u_, v_ = turn_g[:, 0:NN * LA], turn_g[:, NN * LA:2 * NN * LA]
            weight = {n: spread(small(n), [[1, NN], [0, LA]]) for n in ("sre", "sim")}
            ha = "p (h a) -> p h a"
            link(nc.gpsimd.tensor_tensor(u_, u_, amp_g[:], ALU.mult))
            link(nc.gpsimd.tensor_tensor(v_, v_, amp_g[:], ALU.mult))
            link(nc.gpsimd.tensor_tensor(u_.rearrange(ha, a=LA), u_.rearrange(ha, a=LA), weight["sre"], ALU.mult))
            link(nc.gpsimd.tensor_tensor(v_.rearrange(ha, a=LA), v_.rearrange(ha, a=LA), weight["sim"], ALU.mult))
            nc.gpsimd.tensor_tensor(ssm_g[:].rearrange("p h a -> p (h a)"), u_, v_, ALU.subtract).then_inc(s_e, 1)
            for part in range(4, NPART):
                pool.wait_ge(d_b, 64 * part)
                gather_part(part)
                split_w(2 * part - 2, 0)
                split_w(2 * part - 1, 1)
            split_w(10, 0)

            def split_wd(u, j, s):
                pool.wait_ge(wdh_done, u + 1)
                if u < 2:
                    pool.wait_ge(s_e, 2)
                else:
                    pool.wait_ge(down_used, u - 1)
                nc.gpsimd.tensor_tensor(wd_lo[s][:], wd_raw[:, bass.ds(j, 1), :].rearrange("p o c -> p (o c)"), wd_hi[s][:].bitcast(F32),
                                        ALU.subtract).then_inc(wdl_done, 1)

            split_wd(0, 0, 0)
            pool.wait_ge(gu_done, FC)
            for g in range(NG):
                nc.gpsimd.indirect_dma_start(
                    out=bd_raw[:, g, :], out_offset=None, in_=b_d,
                    in_offset=bass.IndirectOffsetOnAxis(ap=rows[:, NPART, g:g + 1], axis=0)).then_inc(d_bd, 16)
            for j in range(1, 5):
                split_wd(j, j, j % 2)
            for g in range(NG):
                pool.wait_ge(bdh_done, g + 1)
                nc.gpsimd.tensor_tensor(bd_lo[:, g, :], bd_raw[:, g, :], bd_hi[:, g, :].bitcast(F32),
                                        ALU.subtract).then_inc(bdl_done, 1)
                split_wd(5 + g, 5 + g, (5 + g) % 2)
            split_wd(9, 9, 1)
            split_wd(10, 10, 0)

        @block.scalar
        def _(act):
            act.wait_ge(zeros_ready, 1)
            nc.scalar.activation(junk[:], zeros[:, 0:1], ACT.Exp)

            def split_w(j, s):
                if isinstance(j, int):
                    act.wait_ge(d_w[s], 16 * (j // 2 + 1))
                if not (isinstance(j, int) and j < 2):
                    act.wait_ge(w_used, j - 1)
                nc.scalar.copy(w_hi[s][:], w_raw[s][:]).then_inc(wh_done, 1)

            def split_b(pair, s):
                act.wait_ge(d_b, 64 * (pair + 1))
                if not (isinstance(pair, int) and pair == 0):
                    act.wait_ge(gu_done, 2 * pair + s - 1)
                nc.scalar.copy(b_hi[s][:], b_raw[:, bass.ds(pair, 1), :, s * 2 * P:(s + 1) * 2 * P].rearrange(
                    "p o g c -> p (o g) c")).then_inc(bh_done, 1)

            def make_silu(j, s):
                act.wait_ge(gu_done, j + 1)
                if not (isinstance(j, int) and j < 2):
                    act.wait_ge(hid_done, j - 1)
                nc.scalar.activation(silu[s][:], banks[:, 4 * s:4 * s + 2, :].rearrange("p h t -> p (h t)"),
                                     ACT.Silu).then_inc(silu_done, 1)

            def split_x(k):
                act.wait_ge(d_x[k], 16)
                nc.scalar.copy(x_hi[:, k, :], x_raw[:, k, :]).then_inc(xh_done, 1)

            act.wait_ge(d_first, 16)
            nc.scalar.copy(by_k(w_hi[0], 0, 1), by_k(w_raw[0], 0, 1)).then_inc(first_hi, 1)
            act.wait_ge(d_x_first, 16)
            nc.scalar.copy(x_hi[:, 0, 0:HT], x_raw[:, 0, 0:HT]).then_inc(first_hi, 1)
            act.wait_ge(d_x[0], 16)
            nc.scalar.copy(x_hi[:, 0, HT:TOK], x_raw[:, 0, HT:TOK]).then_inc(xh_done, 1)
            act.wait_ge(d_w[0], 16)
            nc.scalar.copy(by_k(w_hi[0], 1, KC), by_k(w_raw[0], 1, KC)).then_inc(wh_done, 1)
            for k in range(1, KC):
                split_x(k)
            split_w(1, 1)
            for i in range(4):
                act.wait_ge(tm_done, i + 1)
                hb = slice((i // 2) * HT, (i // 2 + 1) * HT)
                nc.scalar.copy(t_hi[:, i % 2, hb], t_mask[:, i % 2, hb]).then_inc(th_done, 1)
            act.wait_ge(warm_used, 1)
            split_b(0, 0)
            split_b(0, 1)
            split_w(2, 0)
            make_silu(0, 0)
            make_silu(1, 1)
            split_w(3, 1)
            split_b(1, 0)
            split_b(1, 1)
            act.wait_ge(s_rates, 1)
            nc.scalar.activation(small("ea"), small("ar"), ACT.Exp).then_inc(s_exp1, 1)
            nc.scalar.activation(small("tnh"), small("ar"), ACT.Tanh, scale=0.5).then_inc(s_exp1, 1)
            act.wait_ge(s_ampin, 2)
            nc.scalar.activation(amp[:], amp[:], ACT.Exp).then_inc(s_amp, 1)
            nc.scalar.activation(amp_g[:], amp_g[:], ACT.Exp).then_inc(s_amp, 1)
            make_silu(2, 0)
            split_w(4, 0)
            nc.scalar.activation(small("sh"), small("r1"), ACT.Sin, scale=0.5).then_inc(s_exp1, 1)
            nc.scalar.activation(small("sn"), small("r1"), ACT.Sin).then_inc(s_exp1, 1)
            act.wait_ge(s_ang, 1)
            nc.scalar.activation(turn[:], ang[:], ACT.Sin).then_inc(s_sin, 1)
            split_w(5, 1)
            act.wait_ge(s_ang, 2)
            nc.scalar.activation(turn_g[:], ang_g[:], ACT.Sin).then_inc(s_sin, 1)
            split_b(2, 0)
            make_silu(3, 1)
            split_b(2, 1)
            make_silu(4, 0)
            with act.Fori(0, 2) as i:
                act.wait_ge(d_w[0], 16 * (i + 4))
                split_w(2 * i + 6, 0)
                split_b(i + 3, 0)
                make_silu(2 * i + 5, 1)
                act.wait_ge(d_w[1], 16 * (i + 4))
                split_w(2 * i + 7, 1)
                split_b(i + 3, 1)
                make_silu(2 * i + 6, 0)
            split_w(10, 0)
            split_b(5, 0)
            make_silu(9, 1)

            def split_wd(u, j, s):
                if isinstance(u, int) and u in (0, WD_FIRST):
                    act.wait_ge(d_wd[u // WD_FIRST], 16)
                if isinstance(u, int) and u < 2:
                    act.wait_ge(s_e, 2)
                else:
                    act.wait_ge(down_used, u - 1)
                nc.scalar.copy(wd_hi[s][:], wd_raw[:, bass.ds(j, 1), :].rearrange("p o c -> p (o c)")).then_inc(wdh_done, 1)

            def copy_ad(j, s):
                if isinstance(j, int) and j < 2:
                    act.wait_ge(d_ad, 16 * NB)
                    act.wait_ge(bl_done, 8)
                    act.wait_ge(bh_done, 8)
                else:
                    act.wait_ge(down_used, j - 1)
                nc.scalar.copy(ad_rows[s][:].rearrange("p (b r) -> p b r", r=RANK),
                               ad_raw[:, :, bass.ds(j * RANK, RANK)]).then_inc(ad_done, 1)

            def split_ha(j, s):
                if isinstance(j, int) and j == 0:
                    act.wait_ge(w_used, 10)
                elif isinstance(j, int) and j == 1:
                    act.wait_ge(gu_done, FC)
                else:
                    act.wait_ge(down_used, j - 1)
                act.wait_ge(hid_done, j + 1)
                nc.scalar.copy(ha_hi[s][:], hid[:, 0, bass.ds(j * HT, HT)]).then_inc(hh_done, 1)

            def split_a(j, s):
                copy_ad(j, s)
                split_ha(j, s)
                split_wd(j, j, s)

            split_a(0, 0)
            act.wait_ge(gu_done, FC)
            act.wait_ge(hid_done, FC - 2)
            for half in range(2):
                nc.scalar.activation(silu[0][:, half * HT:(half + 1) * HT], banks[:, half, :],
                                     ACT.Silu).then_inc(silu_done, 1)
            for j in range(1, 5):
                split_a(j, j % 2)
            act.wait_ge(d_bd, 16 * NG)
            for g in range(NG):
                nc.scalar.copy(bd_hi[:, g, :], bd_raw[:, g, :]).then_inc(bdh_done, 1)
                split_a(5 + g, (5 + g) % 2)
            split_a(9, 1)
            split_a(10, 0)

            def split_b_unit(j, s):
                if isinstance(j, int) and j < 2:
                    act.wait_ge(w_used, FC)
                else:
                    act.wait_ge(down_used, j + 10)
                nc.scalar.copy(hb_hi[s][:], hid[:, 1, bass.ds(j * HT, HT)]).then_inc(hh_done, 1)

            split_b_unit(0, 0)
            split_wd(FC, 0, 1)
            act.wait_ge(tdm_done, 1)
            nc.scalar.copy(td_hi[:], td_mask[:]).then_inc(tdh_done, 1)
            split_b_unit(1, 1)
            split_wd(FC + 1, 1, 0)
            with act.Fori(0, 4) as i:
                split_b_unit(2 * i + 2, 0)
                split_wd(2 * i + FC + 2, 2 * i + 2, 1)
                split_b_unit(2 * i + 3, 1)
                split_wd(2 * i + FC + 3, 2 * i + 3, 0)
            split_b_unit(10, 0)
            split_wd(2 * FC - 1, FC - 1, 1)

            def copy_sums(t, l0, l1):
                nc.scalar.copy(conv_sb[t % 2][:, l0:l1].rearrange("p (c l) -> p c l", l=P),
                               banks[:, t % 2, l0:l1].rearrange("p (c l) -> p c l", l=P)[:, :, ::-1],
                               ).then_inc(sum_copied, 1)

            for t in range(STEPS):
                act.wait_ge(conv_done, t + 1)
                if t >= 2:
                    act.wait_ge(back_done, t - 1)
                if t < STEPS - 1:
                    copy_sums(t, 0, H)
            for half in range(2):
                copy_sums(STEPS - 1, half * H // 2, (half + 1) * H // 2)

        @block.vector
        def _(dve):
            v = nc.vector
            chain = [0]

            def link(ins):
                chain[0] += 1
                ins.then_inc(dve_chain, 1)
                dve.wait_ge(dve_chain, chain[0])

            def split_x(k):
                dve.wait_ge(xh_done, k + 1)
                v.tensor_tensor(x_lo[:, k, :], x_raw[:, k, :], x_hi[:, k, :].bitcast(F32),
                                ALU.subtract).then_inc(xl_done, 1)

            v.memset(zeros[:], 0.0).then_inc(zeros_ready, 1)
            v.memset(warm[:], 0.0).then_inc(warm_ready, 1)
            def low(dst, raw, hi):
                return v.tensor_tensor(dst, raw, hi.bitcast(F32), ALU.subtract)

            dve.wait_ge(first_hi, 1)
            low(by_k(w_lo[0], 0, 1), by_k(w_raw[0], 0, 1), by_k(w_hi[0], 0, 1)).then_inc(first_lo, 1)
            dve.wait_ge(first_hi, 2)
            low(x_lo[:, 0, 0:HT], x_raw[:, 0, 0:HT], x_hi[:, 0, 0:HT]).then_inc(first_lo, 1)
            dve.wait_ge(xh_done, 1)
            low(x_lo[:, 0, HT:TOK], x_raw[:, 0, HT:TOK], x_hi[:, 0, HT:TOK]).then_inc(xl_done, 1)
            dve.wait_ge(wh_done, 1)
            low(by_k(w_lo[0], 1, KC), by_k(w_raw[0], 1, KC), by_k(w_hi[0], 1, KC)).then_inc(wl_done, 1)
            for k in range(1, KC):
                split_x(k)
            dve.wait_ge(d_ints, 32)
            link(v.tensor_scalar(rows_f[:], ints_sb[:, NB:NB + NG], float(RANK), c_col(C_RANK), ALU.mult, ALU.add))
            for part in range(NPART):
                link(v.tensor_scalar(rows[:, part, :], rows_f[:], float(part * NAD * RANK), None, ALU.add))
            v.tensor_copy(rows[:, NPART, :], rows_f[:]).then_inc(idx_ready, 1)
            v.tensor_copy(block_sb[:], spread(cst[:, C_BLOCK:C_BLOCK + GB], [[PB, GB // PB], [0, NN], [1, PB]])).then_inc(
                block_ready, 1)
            dve.wait_ge(wh_done, 2)
            low(w_lo[1][:], w_raw[1][:], w_hi[1][:]).then_inc(wl_done, 1)

            dve.wait_ge(block_ready, 1)

            def keep_own(dst, src, groups):
                return v.tensor_tensor(
                    dst.rearrange("p (g q c) -> p g q c", g=groups, q=GB // PB),
                    spread(src, [[PB * NN, groups], [0, GB // PB], [1, PB * NN]]),
                    spread(block_sb[:], [[0, groups], [PB * NN, GB // PB], [1, PB * NN]]), ALU.mult)

            def mask_t(i):
                half, gu = i // 2, i % 2
                hb = slice(half * HT, (half + 1) * HT)
                dve.wait_ge(la_done, 2 * (half + 1))
                keep_own(t_mask[:, gu, hb], banks[:, 4 + half, gu * PB * NN * 2:(gu + 1) * PB * NN * 2],
                         2).then_inc(tm_done, 1)
                dve.wait_ge(th_done, i + 1)
                v.tensor_tensor(t_lo[:, gu, hb], t_mask[:, gu, hb], t_hi[:, gu, hb].bitcast(F32),
                                ALU.subtract).then_inc(tl_done, 1)

            mask_t(0)
            mask_t(1)
            mask_t(2)
            mask_t(3)

            def split_b(pair, s_):
                dve.wait_ge(bh_done, 2 * pair + s_ + 1)
                if not (isinstance(pair, int) and pair == 0):
                    dve.wait_ge(gu_done, 2 * pair + s_ - 1)
                v.tensor_tensor(b_lo[s_][:], b_raw[:, bass.ds(pair, 1), :, s_ * 2 * P:(s_ + 1) * 2 * P].rearrange(
                    "p o g c -> p (o g) c"), b_hi[s_][:].bitcast(F32), ALU.subtract).then_inc(bl_done, 1)

            split_b(0, 0)
            split_b(0, 1)

            def make_hid(j, s_):
                dve.wait_ge(silu_done, j + 1)
                v.tensor_tensor(hid[:, :, bass.ds(j * HT, HT)], silu[s_][:].rearrange("p (h t) -> p h t", h=2),
                                banks[:, 4 * s_ + 2:4 * s_ + 4, :], ALU.mult).then_inc(hid_done, 1)

            make_hid(0, 0)
            make_hid(1, 1)
            split_b(1, 0)
            split_b(1, 1)
            link(v.tensor_copy(lens_f[:], ints_sb[:, 0:NB]))
            link(v.tensor_tensor(mask[:], spread(lens_f[:], [[0, KC], [1, NB]]),
                                 spread(cst[:, C_POS:C_POS + KC], [[1, KC], [0, NB]]), ALU.is_gt))

            dve.wait_ge(d_small, 48)
            xx, kk, rr, pp, ee = (small(n, 2) for n in ("ldt", "k0", "r0", "p0", "e0"))
            link(v.tensor_scalar(kk, xx, LOG2E, ROUND, ALU.mult, ALU.add))
            link(v.tensor_scalar(kk, kk, ROUND, -126.0, ALU.subtract, ALU.max))
            link(v.tensor_scalar(kk, kk, 127.0, None, ALU.min))
            link(v.scalar_tensor_tensor(rr, kk, -LN2_HI, xx, ALU.mult, ALU.add))
            link(v.scalar_tensor_tensor(rr, kk, -LN2_LO, rr, ALU.mult, ALU.add))
            link(v.tensor_scalar(pp, rr, 1.0 / math.factorial(7), None, ALU.mult))
            for n in range(6, 0, -1):
                link(v.scalar_tensor_tensor(pp, pp, 1.0 / math.factorial(n), rr, ALU.add, ALU.mult))
            link(v.tensor_scalar(ee.bitcast(I32), kk, 127.0, 2.0 ** 23, ALU.add, ALU.mult))
            link(v.scalar_tensor_tensor(small("dt", 2), pp, 1.0, ee, ALU.add, ALU.mult))

            def reduce_turns(r, x, k, turns=None):
                if turns is None:
                    link(v.tensor_scalar(k, x, INV_2PI, ROUND, ALU.mult, ALU.add))
                    link(v.tensor_scalar(k, k, ROUND, None, ALU.subtract))
                else:
                    link(v.tensor_scalar(k, x, INV_2PI, turns, ALU.mult, ALU.add))
                    link(v.tensor_scalar(k, k, ROUND, ROUND, ALU.add, ALU.subtract))
                link(v.scalar_tensor_tensor(r, k, -PI2_1, x, ALU.mult, ALU.add))
                link(v.scalar_tensor_tensor(r, k, -PI2_2, r, ALU.mult, ALU.add))

            s = small
            link(v.scalar_tensor_tensor(s("ar"), s("are"), -1.0, s("dt"), ALU.mult, ALU.mult))
            link(v.tensor_tensor(s("th"), s("ai"), s("dt"), ALU.mult))
            link(v.tensor_scalar(s("ars"), s("ar"), float(LA), None, ALU.mult))
            reduce_turns(s("r1"), s("th"), s("hk"))
            link(v.tensor_scalar(s("ra"), s("r1"), float(LA), None, ALU.mult))
            v.tensor_scalar(s("r1"), s("r1"), PI_IN, -PI_IN, ALU.min, ALU.max).then_inc(s_rates, 1)
            dve.wait_ge(s_rates, 1)
            reduce_turns(s("ra"), s("ra"), s("hk"))

            def phase(seg, col):
                link(v.tensor_scalar(seg, seg, c_col(col), PI_IN, ALU.add, ALU.min))

            link(v.tensor_tensor(ang[:].rearrange("p (h j) -> p h j", j=LJ), spread(s("ra"), [[1, NN], [0, LJ]]),
                                 spread(cst[:, C_J:C_J + LJ], [[0, NN], [1, LJ]]), ALU.mult))
            reduce_turns(ang[:], ang[:], turn[:], c_col(C_PHE))
            phase(ang[:], C_PHE + 1)
            v.tensor_scalar(ang[:], ang[:], -PI_IN, None, ALU.max).then_inc(s_ang, 1)

            make_hid(2, 0)
            g_len = NN * LA
            for part in range(2):
                link(v.tensor_tensor(ang_g[:, part * g_len:(part + 1) * g_len].rearrange("p (h a) -> p h a", a=LA),
                                     spread(s("r1"), [[1, NN], [0, LA]]),
                                     spread(cst[:, C_J:C_J + LA], [[0, NN], [1, LA]]), ALU.mult))
            for part, col in ((0, C_PHU), (1, C_PHV)):
                seg = slice(part * g_len, (part + 1) * g_len)
                reduce_turns(ang_g[:, seg], ang_g[:, seg], turn_g[:, seg], c_col(col))
                phase(ang_g[:, seg], col + 1)
            v.tensor_scalar(ang_g[:], ang_g[:], -PI_IN, None, ALU.max).then_inc(s_ang, 1)

            dve.wait_ge(s_exp1, 4)
            link(v.scalar_tensor_tensor(s("em"), s("ea"), 1.0, s("tnh"), ALU.add, ALU.mult))
            link(v.scalar_tensor_tensor(s("cm"), s("sh"), -2.0, s("sh"), ALU.mult, ALU.mult))
            link(v.tensor_tensor(s("zre"), s("ea"), s("cm"), ALU.mult))
            link(v.tensor_tensor(s("zre"), s("zre"), s("em"), ALU.add))
            link(v.tensor_tensor(s("zim"), s("ea"), s("sn"), ALU.mult))
            link(v.tensor_tensor(s("q1"), s("are"), s("are"), ALU.mult))
            link(v.tensor_tensor(s("den"), s("ai"), s("ai"), ALU.mult))
            link(v.tensor_tensor(s("den"), s("den"), s("q1"), ALU.add))
            link(v.reciprocal(s("rden"), s("den")))
            link(v.tensor_tensor(s("q1"), s("zim"), s("ai"), ALU.mult))
            link(v.tensor_tensor(s("q2"), s("zre"), s("are"), ALU.mult))
            link(v.tensor_tensor(s("q1"), s("q1"), s("q2"), ALU.subtract))
            link(v.tensor_tensor(s("q3"), s("zim"), s("are"), ALU.mult))
            link(v.tensor_tensor(s("q4"), s("zre"), s("ai"), ALU.mult))
            link(v.tensor_tensor(s("q3"), s("q3"), s("q4"), ALU.add))
            link(v.scalar_tensor_tensor(s("q1"), s("q1"), 2.0, s("rden"), ALU.mult, ALU.mult))
            link(v.scalar_tensor_tensor(s("q3"), s("q3"), -2.0, s("rden"), ALU.mult, ALU.mult))
            link(v.tensor_tensor(s("sre"), s("cr"), s("q1"), ALU.mult))
            link(v.tensor_tensor(s("q2"), s("ci"), s("q3"), ALU.mult))
            link(v.tensor_tensor(s("sre"), s("sre"), s("q2"), ALU.subtract))
            link(v.tensor_tensor(s("sim"), s("cr"), s("q3"), ALU.mult))
            link(v.tensor_tensor(s("q4"), s("ci"), s("q1"), ALU.mult))
            v.tensor_tensor(s("sim"), s("sim"), s("q4"), ALU.add).then_inc(s_cs, 1)

            split_b(2, 0)
            make_hid(3, 1)
            split_b(2, 1)
            make_hid(4, 0)
            dve.wait_ge(s_e, 2)
            with dve.Fori(0, 2) as i:
                split_b(i + 3, 0)
                make_hid(2 * i + 5, 1)
                split_b(i + 3, 1)
                make_hid(2 * i + 6, 0)
            split_b(5, 0)
            make_hid(9, 1)

            def copy_h(j, s_):
                if isinstance(j, int) and j < 2:
                    dve.wait_ge(wl_done, FC)
                else:
                    dve.wait_ge(down_used, j - 1)
                v.tensor_copy(hs[s_][:], hid[:, :, bass.ds(j * HT, HT)]).then_inc(hs_done, 1)

            def split_ha(j, s_):
                dve.wait_ge(hh_done, j + 1)
                v.tensor_tensor(ha_lo[s_][:], hid[:, 0, bass.ds(j * HT, HT)], ha_hi[s_][:].bitcast(F32),
                                ALU.subtract).then_inc(hl_done, 1)

            def split_a(j, s_):
                copy_h(j, s_)
                split_ha(j, s_)

            split_a(0, 0)
            for half in range(2):
                dve.wait_ge(silu_done, FC + half)
                v.tensor_tensor(hid[:, half, (FC - 1) * HT:FC * HT], silu[0][:, half * HT:(half + 1) * HT],
                                banks[:, 2 + half, :], ALU.mult).then_inc(hid_done, 1)
            dve.wait_ge(k_mm, 1)
            v.tensor_tensor(k_sb[:], banks[:, 6, 0:NN // 4 * LA].rearrange("p (h a) -> p h a", a=LA), skip_sb[:],
                            ALU.add).then_inc(k_ready, 1)
            with dve.Fori(0, 5) as i:
                split_a(2 * i + 1, 1)
                split_a(2 * i + 2, 0)

            dve.wait_ge(wdl_done, FC)

            def split_hb(j, s_):
                dve.wait_ge(hh_done, FC + j + 1)
                v.tensor_tensor(hb_lo[s_][:], hid[:, 1, bass.ds(j * HT, HT)], hb_hi[s_][:].bitcast(F32),
                                ALU.subtract).then_inc(hl_done, 1)
                dve.wait_ge(wdh_done, FC + j + 1)
                v.tensor_tensor(wd_lo[1 - s_][:], wd_raw[:, bass.ds(j, 1), :].rearrange("p o c -> p (o c)"),
                                wd_hi[1 - s_][:].bitcast(F32), ALU.subtract).then_inc(wdl_done, 1)

            def residual(half, c, bank):
                dve.wait_ge(y_done, half * KC + c + 1)
                ins = v.tensor_tensor(
                    x1[:, :, c, half * 2 * GB:(half + 1) * 2 * GB].rearrange("p n (q b) -> p q n b", b=PB),
                    banks[:, bank, :].rearrange("p (q n b) -> p q n b", n=NN, b=PB),
                    x_res[:, c, half * HT:(half + 1) * HT].rearrange("p (q n b) -> p q n b", n=NN, b=PB),
                    ALU.add)
                ins.then_inc(x1_done if half else bank_free, 1)

            split_hb(0, 0)
            dve.wait_ge(td_done, 1)
            keep_own(td_mask[:], banks[:, 4, 0:NG * PB * NN], NG).then_inc(tdm_done, 1)
            dve.wait_ge(tdh_done, 1)
            v.tensor_tensor(td_lo[:], td_mask[:], td_hi[:].bitcast(F32), ALU.subtract).then_inc(tdl_done, 1)
            split_hb(1, 1)
            dve.wait_ge(d_xres, 16)
            for c in range(KC):
                split_hb(2 + c, c % 2)
                residual(0, c, c)
            split_hb(6, 0)
            with dve.Fori(0, 2) as i:
                split_hb(2 * i + 7, 1)
                split_hb(2 * i + 8, 0)
            for c in range(KC):
                residual(1, c, 4 + c)

            def add_masked(t, i, c0, c1, bank):
                dve.wait_ge(back_done, i + 1)
                tmp = conv_tmp[t % 2][:, :, c0:c1, :]
                v.tensor_tensor(
                    tmp, banks[:, bank, :].rearrange("p (c n b) -> p n c b", c=KC, n=QN)[:, :, c0:c1, :],
                    spread(mask[:, c0:c1, :], [[0, QN], [NB, c1 - c0], [1, NB]]), ALU.mult).then_inc(bank_free, 1)
                dve.wait_ge(bank_free, KC + i + 1)
                x1n = x1[:, t * QN:(t + 1) * QN, c0:c1, :]
                v.tensor_tensor(x1n, x1n, tmp, ALU.add).then_inc(out_ready, 1)

            for t in range(STEPS - 1):
                add_masked(t, t, 0, KC, 2 + t % 2)
            for half in range(2):
                add_masked(STEPS - 1, STEPS - 1 + half, half * KC // 2, (half + 1) * KC // 2, 3 + half)

        @block.tensor
        def _(pe):
            mm = nc.tensor.matmul

            def three(dst, st_hi, st_lo, mv_hi, mv_lo, start, stop):
                mm(dst, st_hi, mv_hi, start=start, stop=False)
                mm(dst, st_hi, mv_lo, start=False, stop=False)
                return mm(dst, st_lo, mv_hi, start=False, stop=stop)

            def dense(s, half, gu):
                for k in range(KC):
                    c = gu * KC + k
                    hb = slice(half * HT, (half + 1) * HT)
                    last = three(banks[:, 4 * s + 2 * gu + half, :], w_hi[s][:, c, :], w_lo[s][:, c, :],
                                 x_hi[:, k, hb], x_lo[:, k, hb], k == 0, False)
                return last

            def lora(s):
                for half in range(2):
                    for gu in range(2):
                        for gg in range(2):
                            g = 2 * half + gg
                            last = three(banks[:, 4 * s + 2 * gu + half, gg * GT:(gg + 1) * GT],
                                         b_hi[s][:, g, gu * P:(gu + 1) * P], b_lo[s][:, g, gu * P:(gu + 1) * P],
                                         t_hi[:, gu, g * GT:(g + 1) * GT], t_lo[:, gu, g * GT:(g + 1) * GT],
                                         False, gg == 1)
                last.then_inc(gu_done, 1)

            pe.wait_ge(warm_ready, 1)
            for _ in range(WARM):
                last = mm(banks[:, 7, :], warm[:, 0:P], warm[:], start=True, stop=True)
            last.then_inc(warm_used, 1)
            pe.wait_ge(first_hi, 2)
            pe.wait_ge(first_lo, 2)
            for k in range(KC):
                if k == 1:
                    pe.wait_ge(wh_done, 1)
                    pe.wait_ge(wl_done, 1)
                for half in range(2):
                    if k > 0 or half == 1:
                        pe.wait_ge(xh_done, k + 1)
                        pe.wait_ge(xl_done, k + 1)
                    for gu in range(2):
                        c = gu * KC + k
                        hb = slice(half * HT, (half + 1) * HT)
                        last = three(banks[:, 2 * gu + half, :], w_hi[0][:, c, :], w_lo[0][:, c, :],
                                     x_hi[:, k, hb], x_lo[:, k, hb], k == 0, False)
            last.then_inc(w_used, 1)
            for g in range(NG):
                if g < NG - 1:
                    pe.wait_ge(d_agu[g], 16 * GB)
                else:
                    pe.wait_ge(d_agu[g], 8 * GB)
                    pe.wait_ge(d_agu_pool, 8 * GB)
                for gu in range(2):
                    cols = slice((2 * gu + g % 2) * PB * NN, (2 * gu + g % 2 + 1) * PB * NN)
                    for k in range(KC):
                        c = gu * KC + k
                        for q in range(GB // PB):
                            b0 = g * GB + q * PB
                            last = mm(banks[q * PB * RANK:(q + 1) * PB * RANK, 4 + g // 2, cols],
                                      agu_raw[:, b0:b0 + PB, :, c].rearrange("p b r -> p (b r)"), x_raw[:, k, b0 * NN:(b0 + PB) * NN],
                                      start=(k == 0), stop=(k == KC - 1))
                last.then_inc(la_done, 1)
            pe.wait_ge(wh_done, 2)
            pe.wait_ge(wl_done, 2)
            for gu in (1, 0):
                for half in range(2):
                    if gu == 0:
                        pe.wait_ge(tm_done, 2 * half + 2)
                    last = dense(1, half, gu)
            last.then_inc(w_used, 1)
            pe.wait_ge(th_done, 4)
            pe.wait_ge(tl_done, 4)
            for s in range(2):
                pe.wait_ge(bh_done, s + 1)
                pe.wait_ge(bl_done, s + 1)
                lora(s)

            def chunk(j, s):
                pe.wait_ge(wh_done, j + 1)
                pe.wait_ge(wl_done, j + 1)
                pe.wait_ge(hid_done, j - 1)
                for half in range(2):
                    for gu in range(2):
                        last = dense(s, half, gu)
                last.then_inc(w_used, 1)
                pe.wait_ge(bh_done, j + 1)
                pe.wait_ge(bl_done, j + 1)
                lora(s)

            with pe.Fori(0, 4) as i:
                chunk(2 * i + 2, 0)
                chunk(2 * i + 3, 1)
            chunk(10, 0)

            pe.wait_ge(s_e, 2)
            pe.wait_ge(hid_done, 10)
            for h in range(NN // 4):
                for t in range(4):
                    last = mm(banks[t * LJ:(t + 1) * LJ, 6, h * LA:(h + 1) * LA], ssm_e[:, t * 8 + h, :],
                              ssm_g[:, t * 8 + h, :], start=True, stop=True)
            last.then_inc(k_mm, 1)

            def down(s, half_bank, order, mv_hi, mv_lo, s_w, start, waits=()):
                for n, c in enumerate(order):
                    if n < len(waits) and waits[n] is not None:
                        pe.wait_ge(*waits[n])
                    last = three(banks[:, half_bank + c, :], wd_hi[s_w][:, c * P:(c + 1) * P],
                                 wd_lo[s_w][:, c * P:(c + 1) * P], mv_hi, mv_lo, start, False)
                last.then_inc(down_used, 1)

            def unit_a(j, s, first=False, final=False):
                pe.wait_ge(ad_done, j + 1)
                pe.wait_ge(hs_done, j + 1)
                for g in range(NG):
                    for q in range(GB // PB):
                        b0 = g * GB + q * PB
                        last = mm(banks[q * PB * RANK:(q + 1) * PB * RANK, 4, g * PB * NN:(g + 1) * PB * NN],
                                  ad_rows[s][:, b0 * RANK:(b0 + PB) * RANK],
                                  hs[s][:, g // 2, (b0 * NN) % HT:(b0 * NN) % HT + PB * NN],
                                  start=first and g == 0, stop=final and g == NG - 1)
                if final:
                    last.then_inc(td_done, 1)
                pe.wait_ge(hh_done, j + 1)
                pe.wait_ge(hl_done, j + 1)
                pe.wait_ge(wdh_done, j + 1)
                pe.wait_ge(wdl_done, j + 1)
                waits = ((hid_done, FC), None, (hid_done, FC + 1)) if first else ()
                down(s, 0, (0, 2, 1, 3), ha_hi[s][:], ha_lo[s][:], s, first, waits)

            unit_a(0, 0, first=True)
            with pe.Fori(0, 4) as i:
                unit_a(2 * i + 1, 1)
                unit_a(2 * i + 2, 0)
            unit_a(9, 1)
            unit_a(10, 0, final=True)

            def unit_b(j, s, first=False):
                pe.wait_ge(hh_done, FC + j + 1)
                pe.wait_ge(hl_done, FC + j + 1)
                pe.wait_ge(wdh_done, FC + j + 1)
                pe.wait_ge(wdl_done, FC + j + 1)
                waits = ((k_ready, 1), None, (tdm_done, 1)) if first else ()
                down(s, 4, (2, 3, 0, 1), hb_hi[s][:], hb_lo[s][:], 1 - s, first, waits)

            def lora_down(half):
                for c in range(KC):
                    for gg in range(2):
                        g = 2 * half + gg
                        if half == 0 and c == 0:
                            pe.wait_ge(bdh_done, NG)
                            pe.wait_ge(bdl_done, NG)
                        last = three(banks[:, 4 * half + c, gg * GT:(gg + 1) * GT], bd_hi[:, g, c * P:(c + 1) * P],
                                     bd_lo[:, g, c * P:(c + 1) * P], td_hi[:, g * GT:(g + 1) * GT],
                                     td_lo[:, g * GT:(g + 1) * GT], False, gg == 1)
                    last.then_inc(y_done, 1)

            unit_b(0, 0, first=True)
            pe.wait_ge(tdh_done, 1)
            pe.wait_ge(tdl_done, 1)
            lora_down(0)
            with pe.Fori(0, 5) as i:
                unit_b(2 * i + 1, 1)
                unit_b(2 * i + 2, 0)
            lora_down(1)

            def bring_back(t, i, c0, c1, bank):
                pe.wait_ge(sum_copied, i + 1)
                if t >= 2:
                    pe.wait_ge(bank_free, KC + t - 1)
                for c in range(c0, c1):
                    last = nc.tensor.transpose(banks[:, bank, c * P:(c + 1) * P],
                                               conv_sb[t % 2][:, c * P:(c + 1) * P], eye_sb[:])
                last.then_inc(back_done, 1)

            def conv(t):
                q, turn_ = t % NQ, t // NQ
                pe.wait_ge(d_t[q], 16 * (turn_ + 1))
                if t >= 2:
                    pe.wait_ge(sum_copied, t - 1)
                for c in range(KC):
                    if t == 0:
                        pe.wait_ge(x1_done, c + 1)
                    for n in range(QN):
                        last = mm(banks[n * NB:(n + 1) * NB, t % 2, c * P:H], x1[:, t * QN + n, c, :],
                                  toep[q][:, n, 0:H - c * P], start=(c == 0), stop=(c == KC - 1))
                    if t > 0 and c == 1:
                        bring_back(t - 1, t - 1, 0, KC, 2 + (t - 1) % 2)
                last.then_inc(conv_done, 1)

            pe.wait_ge(d_small, 48)
            for t in range(STEPS):
                conv(t)
            for half in range(2):
                bring_back(STEPS - 1, STEPS - 1 + half, half * KC // 2, (half + 1) * KC // 2, 3 + half)


def kernel(x, itok_B_2_6, itok_B_8_3872, L0_cond_W_gate, L0_cond_W_up, L0_cond_W_down, L0_cond_A_gate,
           L0_cond_B_gate, L0_cond_A_up, L0_cond_B_up, L0_cond_A_down, L0_cond_B_down, L1_cond_log_dt,
           L1_cond_C, L1_cond_log_A_real, L1_cond_A_imag, L1_cond_D):
    import concourse.bacc as bacc
    from concourse.bass_utils import run_bass_kernel_spmd

    def pad_f(a, axis, size=FC * P):
        width = [(0, 0)] * a.ndim
        width[axis] = (0, size - a.shape[axis])
        return np.pad(a, width)

    x = np.asarray(x)
    x_t = x.reshape(NB // PB, PB, NN, KC, P).transpose(4, 3, 0, 2, 1).reshape(P, KC, TOK)
    w = np.stack([pad_f(np.asarray(a), 0) for a in (L0_cond_W_gate, L0_cond_W_up)])
    w_gu = w.reshape(2, FC, P, KC, P).transpose(1, 4, 0, 3, 2).reshape(FC, P, 2 * KC, P)
    w_d = pad_f(np.asarray(L0_cond_W_down), 1).T.reshape(FC, P, KC, P)[..., ::-1].transpose(1, 0, 2, 3)
    w_d = w_d.reshape(P, FC, H)
    a = np.stack([np.asarray(L0_cond_A_gate)[0], np.asarray(L0_cond_A_up)[0]])
    a_gu = a.reshape(2, NAD, RANK, KC, P).transpose(1, 4, 2, 0, 3).reshape(NAD, P, RANK * 2 * KC)
    a_d = pad_f(np.asarray(L0_cond_A_down)[0], 2).reshape(NAD, RANK, FC, P).transpose(0, 3, 2, 1)
    a_d = a_d.reshape(NAD, P, FC * RANK)
    b = np.stack([pad_f(np.asarray(m)[0], 1, 2 * NPART * P) for m in (L0_cond_B_gate, L0_cond_B_up)])
    b_gu = b.reshape(2, NAD, NPART, 2, P, RANK).transpose(2, 1, 5, 3, 0, 4).reshape(NPART * NAD * RANK, 4 * P)
    b_d = np.asarray(L0_cond_B_down)[0].transpose(0, 2, 1).reshape(NAD * RANK, KC, P)[..., ::-1]
    b_d = b_d.reshape(NAD * RANK, H)
    idx = np.asarray(itok_B_2_6)
    ints = np.concatenate([np.tile(np.asarray(itok_B_8_3872), (P, 1)),
                           np.repeat(idx.reshape(NG, GB).T, RANK, axis=0)], axis=1)
    c = np.asarray(L1_cond_C)
    rates = np.stack([np.tile(np.asarray(L1_cond_log_dt), (MODES, 1)), np.asarray(L1_cond_log_A_real).T,
                      np.asarray(L1_cond_A_imag).T, c[:, :, 0].T, c[:, :, 1].T], axis=1)
    params = np.concatenate([rates, rates], axis=0).reshape(P, 5 * NN)
    skip = np.zeros((4, LJ, NN // 4, LA), np.float32)
    skip[:, 0, :, 0] = np.asarray(L1_cond_D).reshape(4, NN // 4)
    skip = skip.reshape(P, NN // 4, LA)

    nc = bacc.Bacc("TRN2", target_bir_lowering=False, num_devices=1)
    arrays, args = {}, []
    for name, v in (("x_t", x_t), ("x_rev", x_t[::-1]), ("w_gu", w_gu), ("w_d", w_d), ("a_gu", a_gu), ("a_d", a_d), ("b_gu", b_gu),
                    ("b_d", b_d), ("idx_row", idx.reshape(1, NB)), ("ints", ints), ("params", params),
                    ("skip", skip), ("eye", np.eye(P, dtype=np.float32)), ("consts", constants())):
        v = np.ascontiguousarray(v)
        arrays[name] = v
        args.append(nc.dram_tensor(name, v.shape, mybir.dt.from_np(v.dtype), kind="ExternalInput").ap())
    out = nc.dram_tensor("out", (P, NN, KC, NB), F32, kind="ExternalOutput").ap()
    program(nc, *args, out)
    r = run_bass_kernel_spmd(nc, [arrays], core_ids=[0])
    y = r.results[0]["out"][::-1]
    return y.transpose(3, 1, 2, 0).reshape(NB, NN, H)
```

```python
import math
from contextlib import ExitStack

import numpy as np

import concourse.bass as bass
from concourse import mybir
from concourse.alu_op_type import AluOpType as ALU

F32 = mybir.dt.float32
F32R = mybir.dt.float32r
I32 = mybir.dt.int32
ACT = mybir.ActivationFunctionType

P = 128
NB, NN, H, F = 32, 32, 512, 1376
WARM = 10
WD_FIRST = 3
RANK, NAD = 16, 16
LORA_SCALE = 0.5
FC = -(-F // P)
KC = H // P
GB = P // RANK
NG = NB // GB
GT = GB * NN
TOK = NB * NN
HT = TOK // 2
NPART = (FC + 1) // 2
MODES = 64
PB = 2
LA, LJ = 16, 32
PAD = P
QN = 4
NQ = 4
STEPS = NN // QN
A_SPLIT = NB - 3
X_PIECES = [(0, 0, HT), (0, HT, TOK), (1, 0, HT), (1, HT, TOK)] + [(k, 0, TOK) for k in range(2, KC)]
SBUF0 = 16512

C_J, C_PHE, C_PHU, C_PHV, C_RANK, C_BLOCK = 0, 32, 34, 36, 38, 39
NCONST = C_BLOCK + GB

LOG2E = 1.0 / math.log(2.0)
LN2_HI, LN2_LO = 0.693145751953125, 1.42860676533018518e-06
INV_2PI = 1.0 / (2.0 * math.pi)
PI2_1 = 6.28125
PI2_2 = 2.0 * math.pi - PI2_1
PI_IN = 3.1415925
ROUND = 1.5 * 2.0 ** 23


def constants():
    c = np.zeros((P, NCONST), np.float32)
    p = np.arange(P)
    imag = p // MODES
    c[:, C_J:C_J + LJ] = np.arange(LJ)
    for col, turns in ((C_PHE, (0.25, 0.0)), (C_PHU, (0.25, 0.5)), (C_PHV, (0.0, 0.25))):
        c[:, col] = np.array(turns)[imag]
        c[:, col + 1] = np.array(turns)[imag] * 2.0 * math.pi
    c[:, C_RANK] = p % RANK
    c[:, C_BLOCK:C_BLOCK + GB] = LORA_SCALE * (p[:, None] // RANK == np.arange(GB))
    return c


def program(nc, x_t, x_rev, w_gu, w_d, a_gu, a_d, b_gu, b_d, idx_row, ints, params, skip, eye, pos, consts, out):
    ctx = ExitStack()
    with ctx:
        def sem(name):
            return ctx.enter_context(nc.semaphore(name))

        def at(name, kib, shape, dt=F32):
            return nc.alloc_sbuf_tensor_at(name, shape, dt, offset=SBUF0 + int(kib * 1024))

        ctx.enter_context(nc.sbuf_tensor("slab", [P, (207 * 1024) // 4], F32))

        b_raw = at("b_raw", 0, [P, NPART, NG, 2 * 2 * P])
        x_raw = at("x_raw", 16, [P, KC, TOK])
        agu_raw = at("agu_raw", 32, [P, NB, RANK, 2 * KC])
        ad_raw = at("ad_raw", 0, [P, NB, FC * RANK])
        ad_rows = [at(f"ad_rows{s}", 24 + 4 * s, [P, NB * RANK]) for s in range(2)]
        toep = [at(f"toep{q}", 8 * q, [P, QN, H]) for q in range(NQ)]
        b_hi = [at(f"b_hi{s}", 56 - 8 * s, [P, NG, 2 * P], F32R) for s in range(2)]
        b_lo = [at(f"b_lo{s}", 60 - 8 * s, [P, NG, 2 * P], F32R) for s in range(2)]
        w_hi = [at(f"w_hi{s}", 64 + 8 * s, [P, 2 * KC, P], F32R) for s in range(2)]
        w_lo = [at(f"w_lo{s}", 68 + 8 * s, [P, 2 * KC, P], F32R) for s in range(2)]
        w_raw = [at(f"w_raw{s}", 80 + 4 * s, [P, 2 * KC, P]) for s in range(2)]
        ha_hi = [at("ha_hi0", 72, [P, HT], F32R), at("ha_hi1", 56, [P, HT], F32R)]
        ha_lo = [at("ha_lo0", 76, [P, HT], F32R), at("ha_lo1", 60, [P, HT], F32R)]
        hs = [at(f"hs{s}", 80 + 4 * s, [P, 2, HT]) for s in range(2)]
        hb_hi = [at(f"hb_hi{s}", 64 + 4 * s, [P, HT], F32R) for s in range(2)]
        hb_lo = [at(f"hb_lo{s}", 66 + 4 * s, [P, HT], F32R) for s in range(2)]
        wd_raw = at("wd_raw", 32, [P, FC, H])
        conv_sb = [at(f"conv_sb{s}", 84 + 2 * s, [P, H]) for s in range(2)]
        t_mask = at("t_mask", 88, [P, 2, TOK])
        silu = [at(f"silu{s}", 88 + 4 * s, [P, TOK]) for s in range(2)]
        td_mask = at("td_mask", 88, [P, TOK])
        k_sb = at("k_sb", 92, [P, NN // 4, LA])
        ssm_e = at("ssm_e", 96, [P, NN, LJ])
        pos_sb = at("pos_sb", 96, [P, H])
        ssm_g = at("ssm_g", 100, [P, NN, LA])
        hid = at("hid", 102, [P, 2, FC * HT])
        ang = at("ang", 134, [P, NN * LJ])
        turn = at("turn", 138, [P, NN * LJ])
        amp = at("amp", 142, [P, NN * LJ])
        x1 = at("x1", 102, [P, NN, KC, NB])
        x_hi = at("x_hi", 146, [P, KC, TOK], F32R)
        x_lo = at("x_lo", 162, [P, KC, TOK], F32R)
        td_hi = at("td_hi", 146, [P, TOK], F32R)
        td_lo = at("td_lo", 150, [P, TOK], F32R)
        bd_raw = at("bd_raw", 154, [P, NG, H])
        bd_hi = at("bd_hi", 162, [P, NG, H], F32R)
        bd_lo = at("bd_lo", 170, [P, NG, H], F32R)
        t_hi = at("t_hi", 178, [P, 2, TOK], F32R)
        t_lo = at("t_lo", 186, [P, 2, TOK], F32R)
        x_res = at("x_res", 178, [P, KC, TOK])
        sm = at("sm", 194, [P, 40, NN])
        wd_hi = [at(f"wd_hi{s}", 194 + 4 * s, [P, H], F32R) for s in range(2)]
        wd_lo = [at(f"wd_lo{s}", 196 + 4 * s, [P, H], F32R) for s in range(2)]
        cst = at("cst", 202, [P, NCONST])
        ints_sb = at("ints_sb", 202.25, [P, 1 + NG], I32)
        idx_sb = at("idx_sb", 202.5, [1, NB], I32)
        rows_f = at("rows_f", 203, [P, NG])
        rows = at("rows", 203.125, [P, NPART + 1, NG], I32)
        len_f = at("len_f", 203.25, [P, 1])
        zeros = at("zeros", 204, [NN, PAD])
        junk = at("junk", 204.5, [NN, 1])
        block_sb = at("block_sb", 205, [P, GB // PB, NN, PB])
        skip_sb = at("skip_sb", 206, [P, NN // 4, LA])
        eye_sb = at("eye_sb", 206.5, [P, P])
        ang_g = at("ang_g", 114, [P, 2 * NN * LA])
        turn_g = at("turn_g", 118, [P, 2 * NN * LA])
        warm = at("warm", 56, [P, P])
        amp_g = at("amp_g", 199, [P, NN * LA])

        banks = ctx.enter_context(nc.psum_tensor("banks", [P, 8, HT], F32))

        k_pad = nc.dram_tensor("k_pad", (NN, PAD + H), F32, kind="Internal").ap()

        d_ints = sem("d_ints")
        d_small = sem("d_small")
        d_idx = sem("d_idx")
        d_first = sem("d_first")
        d_x = [sem(f"d_x{i}") for i in range(len(X_PIECES))]
        d_w = [sem(f"d_w{s}") for s in range(2)]
        d_agu = [sem(f"d_agu{g}") for g in range(NG)]
        d_agu_pool = sem("d_agu_pool")
        d_b = sem("d_b")
        d_ad = sem("d_ad")
        d_bd = sem("d_bd")
        d_wd = [sem(f"d_wd{s}") for s in range(2)]
        d_xres = sem("d_xres")
        d_kpad = sem("d_kpad")
        d_t = [sem(f"d_t{q}") for q in range(NQ)]
        d_pos = sem("d_pos")
        d_out = sem("d_out")
        idx_ready = sem("idx_ready")
        zeros_ready = sem("zeros_ready")
        block_ready = sem("block_ready")
        warm_ready = sem("warm_ready")
        warm_used = sem("warm_used")
        first_hi = sem("first_hi")
        first_lo = sem("first_lo")
        xh_done = sem("xh_done")
        xl_done = sem("xl_done")
        la_done = sem("la_done")
        tm_done = sem("tm_done")
        th_done = sem("th_done")
        tl_done = sem("tl_done")
        wh_done = sem("wh_done")
        wl_done = sem("wl_done")
        bh_done = sem("bh_done")
        bl_done = sem("bl_done")
        w_used = sem("w_used")
        gu_done = sem("gu_done")
        silu_done = sem("silu_done")
        hid_done = sem("hid_done")
        hh_done = sem("hh_done")
        hl_done = sem("hl_done")
        wdh_done = sem("wdh_done")
        wdl_done = sem("wdl_done")
        ad_done = sem("ad_done")
        hs_done = sem("hs_done")
        down_used = sem("down_used")
        td_done = sem("td_done")
        tdm_done = sem("tdm_done")
        tdh_done = sem("tdh_done")
        tdl_done = sem("tdl_done")
        bdh_done = sem("bdh_done")
        bdl_done = sem("bdl_done")
        y_done = sem("y_done")
        x1_done = sem("x1_done")
        conv_done = sem("conv_done")
        sum_masked = sem("sum_masked")
        back_done = sem("back_done")
        out_ready = sem("out_ready")
        k_mm = sem("k_mm")
        k_ready = sem("k_ready")
        dve_chain = sem("dve_chain")
        pool_chain = sem("pool_chain")
        s_rates = sem("s_rates")
        s_exp1 = sem("s_exp1")
        s_cs = sem("s_cs")
        s_ampin = sem("s_ampin")
        s_amp = sem("s_amp")
        s_ang = sem("s_ang")
        s_sin = sem("s_sin")
        s_e = sem("s_e")

        block = ctx.enter_context(nc.Block())

        def by_k(w, k0, k1):
            return w[:].rearrange("p (g k) f -> p g k f", k=KC)[:, :, k0:k1, :]

        def spread(ap, dims):
            return bass.AP(tensor=ap.tensor, offset=ap.offset, ap=[list(ap.ap[0])] + dims)

        names = ("ldt lar ai cr ci k0 k1 r0 r_1 p0 p1 e0 e1 dt are ar th r1 ra ea tnh sh sn em cm zre zim den rden "
                 "q1 q2 q3 q4 sre sim ars hk").split()
        slot = {name: i for i, name in enumerate(names)}

        def small(name, width=1):
            return sm[:, slot[name]:slot[name] + width, :].rearrange("p a b -> p (a b)")

        def c_col(i):
            return cst[:, i:i + 1]

        @block.sync
        def _(sp):
            def load_toeplitz(q, turn_):
                first = k_pad[0:1, 0:1]
                src = bass.AP(tensor=first.tensor, offset=(turn_ * NQ + q) * QN * (PAD + H) + PAD - (P - 1),
                              ap=[[1, P], [PAD + H, QN], [1, H]])
                sp.dma_start(toep[q][:], src).then_inc(d_t[q], 16)

            sp.dma_start(by_k(w_raw[0], 0, 1), by_k(w_gu[0], 0, 1)).then_inc(d_first, 16)
            def load_x(pieces):
                for i in pieces:
                    k, t0, t1 = X_PIECES[i]
                    sp.dma_start(x_raw[:, k, t0:t1], x_t[:, k, t0:t1]).then_inc(d_x[i], 16)

            load_x((0, 1))
            sp.dma_start(idx_sb[:], idx_row).then_inc(d_idx, 16)
            sp.dma_start(by_k(w_raw[0], 1, KC), by_k(w_gu[0], 1, KC)).then_inc(d_w[0], 16)
            load_x(range(2, len(X_PIECES)))
            sp.wait_ge(d_idx, 16)

            def gather_a(batches):
                _, ads = nc.values_load_multi_w_load_instructions(
                    idx_sb[0:1, batches], engines=[mybir.EngineType.SP], min_val=0, max_val=NAD - 1,
                    skip_runtime_bounds_check_because="an adaptor's index")
                for b, ad in zip(range(batches.start, batches.stop), ads):
                    sp.dma_start(agu_raw[:, b:b + 1, :, :].rearrange("p b r c -> p b (r c)"),
                                 a_gu[bass.ds(ad, 1), :, :].rearrange("o p c -> p o c")).then_inc(d_agu[b // GB], 16)

            gather_a(slice(0, GB))
            sp.dma_start(ints_sb[:], ints).then_inc(d_ints, 16)
            sp.dma_start(cst[:], consts).then_inc(d_ints, 16)
            sp.dma_start(w_raw[1][:], w_gu[1]).then_inc(d_w[1], 16)
            gather_a(slice(2 * GB, 3 * GB))
            gather_a(slice(A_SPLIT, NB))
            sp.dma_start(sm[:, 0:5, :].rearrange("p a b -> p (a b)"), params).then_inc(d_small, 16)
            sp.dma_start(skip_sb[:], skip).then_inc(d_small, 16)
            sp.dma_start(eye_sb[:], eye).then_inc(d_small, 16)

            def load_w(j, s):
                sp.wait_ge(wh_done, j - 1)
                sp.wait_ge(wl_done, j - 1)
                sp.dma_start(w_raw[s][:], w_gu[bass.ds(j, 1)].rearrange("o p c f -> p (o c) f")).then_inc(d_w[s], 16)

            with sp.Fori(0, 3) as i:
                load_w(2 * i + 2, 0)
                load_w(2 * i + 3, 1)
            load_w(8, 0)
            sp.wait_ge(bh_done, 6)
            sp.wait_ge(bl_done, 6)
            with sp.Fori(0, NG) as g:
                _, ads = nc.values_load_multi_w_load_instructions(
                    idx_sb[0:1, bass.ds(g * GB, GB)], engines=[mybir.EngineType.SP], min_val=0, max_val=NAD - 1,
                    skip_runtime_bounds_check_because="an adaptor's index")
                for i, ad in enumerate(ads):
                    sp.dma_start(ad_raw[:, bass.ds(g * GB + i, 1), :],
                                 a_d[bass.ds(ad, 1), :, :].rearrange("o p c -> p o c")).then_inc(d_ad, 16)
            load_w(9, 1)
            load_w(10, 0)

            sp.wait_ge(bh_done, FC)
            sp.wait_ge(bl_done, FC)
            sp.wait_ge(gu_done, FC - 1)
            sp.dma_start(wd_raw[:, 0:WD_FIRST, :], w_d[:, 0:WD_FIRST, :]).then_inc(d_wd[0], 16)
            sp.dma_start(wd_raw[:, WD_FIRST:FC, :], w_d[:, WD_FIRST:FC, :]).then_inc(d_wd[1], 16)
            sp.wait_ge(gu_done, FC)
            sp.dma_start(x_res[:], x_rev).then_inc(d_xres, 16)
            sp.wait_ge(zeros_ready, 1)
            sp.dma_start(k_pad[:, 0:PAD], zeros[:]).then_inc(d_kpad, 16)
            sp.wait_ge(k_ready, 1)
            for t in range(4):
                sp.dma_start(k_pad[t * 8:(t + 1) * 8, PAD:PAD + H].rearrange("h (j a) -> j h a", a=LA),
                             k_sb[t * LJ:(t + 1) * LJ]).then_inc(d_kpad, 16)
            sp.dma_start(pos_sb[:], pos).then_inc(d_pos, 16)
            sp.wait_ge(d_kpad, 16 * 5)
            sp.wait_ge(down_used, FC)
            for q in range(NQ):
                load_toeplitz(q, 0)
            for q in range(NQ):
                sp.wait_ge(conv_done, q + 1)
                load_toeplitz(q, 1)
            for t in range(STEPS):
                sp.wait_ge(out_ready, t + 1 if t < STEPS - 1 else STEPS + 1)
                sp.dma_start(out[:, t * QN:(t + 1) * QN, :, :], x1[:, t * QN:(t + 1) * QN, :, :]).then_inc(d_out, 16)
            sp.wait_ge(d_out, 16 * STEPS)

        @block.gpsimd
        def _(pool):
            chain = [0]

            def link(ins):
                chain[0] += 1
                ins.then_inc(pool_chain, 1)
                pool.wait_ge(pool_chain, chain[0])

            def gather_part(part):
                for g in range(NG):
                    nc.gpsimd.indirect_dma_start(
                        out=b_raw[:, part, g, :], out_offset=None, in_=b_gu,
                        in_offset=bass.IndirectOffsetOnAxis(ap=rows[:, part, g:g + 1], axis=0)).then_inc(d_b, 16)

            def split_w(j, s):
                pool.wait_ge(wh_done, j + 1)
                if not (isinstance(j, int) and j < 2):
                    pool.wait_ge(w_used, j - 1)
                nc.gpsimd.tensor_tensor(w_lo[s][:], w_raw[s][:], w_hi[s][:].bitcast(F32),
                                        ALU.subtract).then_inc(wl_done, 1)

            pool.wait_ge(d_idx, 16)
            for batches in (slice(GB, 2 * GB), slice(NB - GB, A_SPLIT)):
                _, ads = nc.values_load_multi_w_load_instructions(
                    idx_sb[0:1, batches], engines=[mybir.EngineType.Pool], min_val=0, max_val=NAD - 1,
                    skip_runtime_bounds_check_because="an adaptor's index")
                for b, ad in zip(range(batches.start, batches.stop), ads):
                    nc.gpsimd.dma_start(agu_raw[:, b:b + 1, :, :].rearrange("p b r c -> p b (r c)"),
                                        a_gu[bass.ds(ad, 1), :, :].rearrange("o p c -> p o c")
                                        ).then_inc(d_agu[1] if b < 2 * GB else d_agu_pool, 16)
            pool.wait_ge(idx_ready, 1)
            pool.wait_ge(d_agu[NG - 1], 16 * (NB - A_SPLIT))
            gather_part(0)
            pool.wait_ge(d_b, 64)
            gather_part(1)
            pool.wait_ge(d_b, 128)
            pool.wait_ge(la_done, NG)
            pool.wait_ge(xh_done, len(X_PIECES))
            pool.wait_ge(xl_done, len(X_PIECES))
            pool.wait_ge(wl_done, 2)
            split_w(2, 0)
            gather_part(2)
            split_w(3, 1)
            pool.wait_ge(d_b, 64 * 3)
            gather_part(3)
            pool.wait_ge(s_rates, 1)
            nc.gpsimd.tensor_tensor(
                amp[:].rearrange("p (h j) -> p h j", j=LJ), spread(small("ars"), [[1, NN], [0, LJ]]),
                spread(cst[:, C_J:C_J + LJ], [[0, NN], [1, LJ]]), ALU.mult).then_inc(s_ampin, 1)
            nc.gpsimd.tensor_tensor(
                amp_g[:].rearrange("p (h a) -> p h a", a=LA), spread(small("ar"), [[1, NN], [0, LA]]),
                spread(cst[:, C_J:C_J + LA], [[0, NN], [1, LA]]), ALU.mult).then_inc(s_ampin, 1)
            split_w(4, 0)
            pool.wait_ge(s_amp, 1)
            pool.wait_ge(s_sin, 1)
            nc.gpsimd.tensor_tensor(ssm_e[:].rearrange("p h j -> p (h j)"), turn[:], amp[:],
                                    ALU.mult).then_inc(s_e, 1)
            split_w(5, 1)
            pool.wait_ge(s_amp, 2)
            pool.wait_ge(s_sin, 2)
            pool.wait_ge(s_cs, 1)
            u_, v_ = turn_g[:, 0:NN * LA], turn_g[:, NN * LA:2 * NN * LA]
            weight = {n: spread(small(n), [[1, NN], [0, LA]]) for n in ("sre", "sim")}
            ha = "p (h a) -> p h a"
            link(nc.gpsimd.tensor_tensor(u_, u_, amp_g[:], ALU.mult))
            link(nc.gpsimd.tensor_tensor(v_, v_, amp_g[:], ALU.mult))
            link(nc.gpsimd.tensor_tensor(u_.rearrange(ha, a=LA), u_.rearrange(ha, a=LA), weight["sre"], ALU.mult))
            link(nc.gpsimd.tensor_tensor(v_.rearrange(ha, a=LA), v_.rearrange(ha, a=LA), weight["sim"], ALU.mult))
            nc.gpsimd.tensor_tensor(ssm_g[:].rearrange("p h a -> p (h a)"), u_, v_, ALU.subtract).then_inc(s_e, 1)
            for part in range(4, NPART):
                pool.wait_ge(d_b, 64 * part)
                gather_part(part)
                split_w(2 * part - 2, 0)
                split_w(2 * part - 1, 1)
            split_w(10, 0)

            def split_wd(u, j, s):
                pool.wait_ge(wdh_done, u + 1)
                if u < 2:
                    pool.wait_ge(s_e, 2)
                else:
                    pool.wait_ge(down_used, u - 1)
                nc.gpsimd.tensor_tensor(wd_lo[s][:], wd_raw[:, j, :], wd_hi[s][:].bitcast(F32),
                                        ALU.subtract).then_inc(wdl_done, 1)

            def gather_bd(groups):
                for g in groups:
                    nc.gpsimd.indirect_dma_start(
                        out=bd_raw[:, g, :], out_offset=None, in_=b_d,
                        in_offset=bass.IndirectOffsetOnAxis(ap=rows[:, NPART, g:g + 1], axis=0)).then_inc(d_bd, 16)

            split_wd(0, 0, 0)
            pool.wait_ge(gu_done, FC)
            gather_bd((0, 1))
            split_wd(1, 1, 1)
            gather_bd((2,))
            split_wd(2, 2, 0)
            gather_bd((3,))
            split_wd(3, 3, 1)
            split_wd(4, 4, 0)
            for g in range(NG):
                pool.wait_ge(bdh_done, g + 1)
                nc.gpsimd.tensor_tensor(bd_lo[:, g, :], bd_raw[:, g, :], bd_hi[:, g, :].bitcast(F32),
                                        ALU.subtract).then_inc(bdl_done, 1)
                split_wd(5 + g, 5 + g, (5 + g) % 2)
            split_wd(9, 9, 1)
            split_wd(10, 10, 0)

        @block.scalar
        def _(act):
            act.wait_ge(zeros_ready, 1)
            nc.scalar.activation(junk[:], zeros[:, 0:1], ACT.Exp)

            def split_w(j, s):
                if isinstance(j, int):
                    act.wait_ge(d_w[s], 16 * (j // 2 + 1))
                if not (isinstance(j, int) and j < 2):
                    act.wait_ge(w_used, j - 1)
                nc.scalar.copy(w_hi[s][:], w_raw[s][:]).then_inc(wh_done, 1)

            def split_b(pair, s):
                act.wait_ge(d_b, 64 * (pair + 1))
                if not (isinstance(pair, int) and pair == 0):
                    act.wait_ge(gu_done, 2 * pair + s - 1)
                nc.scalar.copy(b_hi[s][:], b_raw[:, bass.ds(pair, 1), :, s * 2 * P:(s + 1) * 2 * P].rearrange(
                    "p o g c -> p (o g) c")).then_inc(bh_done, 1)

            def make_silu(j, s):
                act.wait_ge(gu_done, j + 1)
                if not (isinstance(j, int) and j < 2):
                    act.wait_ge(hid_done, j - 1)
                nc.scalar.activation(silu[s][:], banks[:, 4 * s:4 * s + 2, :].rearrange("p h t -> p (h t)"),
                                     ACT.Silu).then_inc(silu_done, 1)

            def split_x(pieces):
                for i in pieces:
                    k, t0, t1 = X_PIECES[i]
                    act.wait_ge(d_x[i], 16)
                    nc.scalar.copy(x_hi[:, k, t0:t1], x_raw[:, k, t0:t1]).then_inc(xh_done, 1)

            act.wait_ge(d_first, 16)
            nc.scalar.copy(by_k(w_hi[0], 0, 1), by_k(w_raw[0], 0, 1)).then_inc(first_hi, 1)
            split_x((0, 1))
            act.wait_ge(d_w[0], 16)
            nc.scalar.copy(by_k(w_hi[0], 1, KC), by_k(w_raw[0], 1, KC)).then_inc(wh_done, 1)
            split_x(range(2, len(X_PIECES)))
            split_w(1, 1)
            for i in range(4):
                act.wait_ge(tm_done, i + 1)
                hb = slice((i // 2) * HT, (i // 2 + 1) * HT)
                nc.scalar.copy(t_hi[:, i % 2, hb], t_mask[:, i % 2, hb]).then_inc(th_done, 1)
            act.wait_ge(warm_used, 1)
            split_b(0, 0)
            split_b(0, 1)
            split_w(2, 0)
            make_silu(0, 0)
            make_silu(1, 1)
            split_w(3, 1)
            split_b(1, 0)
            split_b(1, 1)
            act.wait_ge(s_rates, 1)
            nc.scalar.activation(small("ea"), small("ar"), ACT.Exp).then_inc(s_exp1, 1)
            nc.scalar.activation(small("tnh"), small("ar"), ACT.Tanh, scale=0.5).then_inc(s_exp1, 1)
            act.wait_ge(s_ampin, 2)
            nc.scalar.activation(amp[:], amp[:], ACT.Exp).then_inc(s_amp, 1)
            nc.scalar.activation(amp_g[:], amp_g[:], ACT.Exp).then_inc(s_amp, 1)
            make_silu(2, 0)
            split_w(4, 0)
            nc.scalar.activation(small("sh"), small("r1"), ACT.Sin, scale=0.5).then_inc(s_exp1, 1)
            nc.scalar.activation(small("sn"), small("r1"), ACT.Sin).then_inc(s_exp1, 1)
            act.wait_ge(s_ang, 1)
            nc.scalar.activation(turn[:], ang[:], ACT.Sin).then_inc(s_sin, 1)
            split_w(5, 1)
            act.wait_ge(s_ang, 2)
            nc.scalar.activation(turn_g[:], ang_g[:], ACT.Sin).then_inc(s_sin, 1)
            split_b(2, 0)
            make_silu(3, 1)
            split_b(2, 1)
            make_silu(4, 0)
            with act.Fori(0, 2) as i:
                act.wait_ge(d_w[0], 16 * (i + 4))
                split_w(2 * i + 6, 0)
                split_b(i + 3, 0)
                make_silu(2 * i + 5, 1)
                act.wait_ge(d_w[1], 16 * (i + 4))
                split_w(2 * i + 7, 1)
                split_b(i + 3, 1)
                make_silu(2 * i + 6, 0)
            split_w(10, 0)
            split_b(5, 0)
            make_silu(9, 1)

            def split_wd(u, j, s):
                if isinstance(u, int) and u in (0, WD_FIRST):
                    act.wait_ge(d_wd[u // WD_FIRST], 16)
                if isinstance(u, int) and u < 2:
                    act.wait_ge(s_e, 2)
                else:
                    act.wait_ge(down_used, u - 1)
                nc.scalar.copy(wd_hi[s][:], wd_raw[:, bass.ds(j, 1), :].rearrange("p o c -> p (o c)")
                               ).then_inc(wdh_done, 1)

            def copy_ad(j, s):
                if isinstance(j, int) and j < 2:
                    act.wait_ge(d_ad, 16 * NB)
                    act.wait_ge(bl_done, 8)
                    act.wait_ge(bh_done, 8)
                else:
                    act.wait_ge(down_used, j - 1)
                nc.scalar.copy(ad_rows[s][:].rearrange("p (b r) -> p b r", r=RANK),
                               ad_raw[:, :, bass.ds(j * RANK, RANK)]).then_inc(ad_done, 1)

            def split_ha(j, s):
                if isinstance(j, int) and j == 0:
                    act.wait_ge(w_used, 10)
                elif isinstance(j, int) and j == 1:
                    act.wait_ge(gu_done, FC)
                else:
                    act.wait_ge(down_used, j - 1)
                act.wait_ge(hid_done, j + 1)
                nc.scalar.copy(ha_hi[s][:], hid[:, 0, bass.ds(j * HT, HT)]).then_inc(hh_done, 1)

            def split_a(j, s):
                copy_ad(j, s)
                split_ha(j, s)
                split_wd(j, j, s)

            split_a(0, 0)
            act.wait_ge(gu_done, FC)
            act.wait_ge(hid_done, FC - 2)
            for half in range(2):
                nc.scalar.activation(silu[0][:, half * HT:(half + 1) * HT], banks[:, half, :],
                                     ACT.Silu).then_inc(silu_done, 1)
            for j in range(1, 5):
                split_a(j, j % 2)
            act.wait_ge(d_bd, 16 * NG)
            for g in range(NG):
                nc.scalar.copy(bd_hi[:, g, :], bd_raw[:, g, :]).then_inc(bdh_done, 1)
                split_a(5 + g, (5 + g) % 2)
            split_a(9, 1)
            split_a(10, 0)

            def split_b_unit(j, s):
                if isinstance(j, int) and j < 2:
                    act.wait_ge(w_used, FC)
                else:
                    act.wait_ge(down_used, j + 10)
                nc.scalar.copy(hb_hi[s][:], hid[:, 1, bass.ds(j * HT, HT)]).then_inc(hh_done, 1)

            split_b_unit(0, 0)
            split_wd(FC, 0, 1)
            act.wait_ge(tdm_done, 1)
            nc.scalar.copy(td_hi[:], td_mask[:]).then_inc(tdh_done, 1)
            split_b_unit(1, 1)
            split_wd(FC + 1, 1, 0)
            with act.Fori(0, 4) as i:
                split_b_unit(2 * i + 2, 0)
                split_wd(2 * i + FC + 2, 2 * i + 2, 1)
                split_b_unit(2 * i + 3, 1)
                split_wd(2 * i + FC + 3, 2 * i + 3, 0)
            split_b_unit(10, 0)
            split_wd(2 * FC - 1, FC - 1, 1)

        @block.vector
        def _(dve):
            v = nc.vector
            chain = [0]

            def link(ins):
                chain[0] += 1
                ins.then_inc(dve_chain, 1)
                dve.wait_ge(dve_chain, chain[0])

            v.memset(warm[:], 0.0).then_inc(warm_ready, 1)
            v.memset(zeros[:], 0.0).then_inc(zeros_ready, 1)
            def low(dst, raw, hi):
                return v.tensor_tensor(dst, raw, hi.bitcast(F32), ALU.subtract)

            def split_x(pieces):
                for i in pieces:
                    k, t0, t1 = X_PIECES[i]
                    dve.wait_ge(xh_done, i + 1)
                    low(x_lo[:, k, t0:t1], x_raw[:, k, t0:t1], x_hi[:, k, t0:t1]).then_inc(xl_done, 1)

            dve.wait_ge(first_hi, 1)
            low(by_k(w_lo[0], 0, 1), by_k(w_raw[0], 0, 1), by_k(w_hi[0], 0, 1)).then_inc(first_lo, 1)
            split_x((0, 1))
            dve.wait_ge(wh_done, 1)
            low(by_k(w_lo[0], 1, KC), by_k(w_raw[0], 1, KC), by_k(w_hi[0], 1, KC)).then_inc(wl_done, 1)
            split_x(range(2, len(X_PIECES)))
            dve.wait_ge(d_ints, 32)
            link(v.tensor_scalar(rows_f[:], ints_sb[:, 1:1 + NG], float(RANK), c_col(C_RANK), ALU.mult, ALU.add))
            for part in range(NPART):
                link(v.tensor_scalar(rows[:, part, :], rows_f[:], float(part * NAD * RANK), None, ALU.add))
            v.tensor_copy(rows[:, NPART, :], rows_f[:]).then_inc(idx_ready, 1)
            v.tensor_copy(block_sb[:], spread(cst[:, C_BLOCK:C_BLOCK + GB], [[PB, GB // PB], [0, NN], [1, PB]])
                          ).then_inc(block_ready, 1)
            dve.wait_ge(wh_done, 2)
            low(w_lo[1][:], w_raw[1][:], w_hi[1][:]).then_inc(wl_done, 1)

            dve.wait_ge(block_ready, 1)

            def keep_own(dst, src, groups):
                return v.tensor_tensor(
                    dst.rearrange("p (g q c) -> p g q c", g=groups, q=GB // PB),
                    spread(src, [[PB * NN, groups], [0, GB // PB], [1, PB * NN]]),
                    spread(block_sb[:], [[0, groups], [PB * NN, GB // PB], [1, PB * NN]]), ALU.mult)

            def mask_t(i):
                half, gu = i // 2, i % 2
                hb = slice(half * HT, (half + 1) * HT)
                dve.wait_ge(la_done, 2 * (half + 1))
                keep_own(t_mask[:, gu, hb], banks[:, 4 + half, gu * PB * NN * 2:(gu + 1) * PB * NN * 2],
                         2).then_inc(tm_done, 1)
                dve.wait_ge(th_done, i + 1)
                v.tensor_tensor(t_lo[:, gu, hb], t_mask[:, gu, hb], t_hi[:, gu, hb].bitcast(F32),
                                ALU.subtract).then_inc(tl_done, 1)

            mask_t(0)
            mask_t(1)
            mask_t(2)
            mask_t(3)

            def split_b(pair, s_):
                dve.wait_ge(bh_done, 2 * pair + s_ + 1)
                if not (isinstance(pair, int) and pair == 0):
                    dve.wait_ge(gu_done, 2 * pair + s_ - 1)
                v.tensor_tensor(b_lo[s_][:], b_raw[:, bass.ds(pair, 1), :, s_ * 2 * P:(s_ + 1) * 2 * P].rearrange(
                    "p o g c -> p (o g) c"), b_hi[s_][:].bitcast(F32), ALU.subtract).then_inc(bl_done, 1)

            split_b(0, 0)
            split_b(0, 1)

            def make_hid(j, s_):
                dve.wait_ge(silu_done, j + 1)
                v.tensor_tensor(hid[:, :, bass.ds(j * HT, HT)], silu[s_][:].rearrange("p (h t) -> p h t", h=2),
                                banks[:, 4 * s_ + 2:4 * s_ + 4, :], ALU.mult).then_inc(hid_done, 1)

            make_hid(0, 0)
            make_hid(1, 1)
            split_b(1, 0)
            split_b(1, 1)
            link(v.tensor_copy(len_f[:], ints_sb[:, 0:1]))

            dve.wait_ge(d_small, 48)
            xx, kk, rr, pp, ee = (small(n, 2) for n in ("ldt", "k0", "r0", "p0", "e0"))
            link(v.tensor_scalar(kk, xx, LOG2E, ROUND, ALU.mult, ALU.add))
            link(v.tensor_scalar(kk, kk, ROUND, -126.0, ALU.subtract, ALU.max))
            link(v.tensor_scalar(kk, kk, 127.0, None, ALU.min))
            link(v.scalar_tensor_tensor(rr, kk, -LN2_HI, xx, ALU.mult, ALU.add))
            link(v.scalar_tensor_tensor(rr, kk, -LN2_LO, rr, ALU.mult, ALU.add))
            link(v.tensor_scalar(pp, rr, 1.0 / math.factorial(7), None, ALU.mult))
            for n in range(6, 0, -1):
                link(v.scalar_tensor_tensor(pp, pp, 1.0 / math.factorial(n), rr, ALU.add, ALU.mult))
            link(v.tensor_scalar(ee.bitcast(I32), kk, 127.0, 2.0 ** 23, ALU.add, ALU.mult))
            link(v.scalar_tensor_tensor(small("dt", 2), pp, 1.0, ee, ALU.add, ALU.mult))

            def reduce_turns(r, x, k, turns=None):
                if turns is None:
                    link(v.tensor_scalar(k, x, INV_2PI, ROUND, ALU.mult, ALU.add))
                    link(v.tensor_scalar(k, k, ROUND, None, ALU.subtract))
                else:
                    link(v.tensor_scalar(k, x, INV_2PI, turns, ALU.mult, ALU.add))
                    link(v.tensor_scalar(k, k, ROUND, ROUND, ALU.add, ALU.subtract))
                link(v.scalar_tensor_tensor(r, k, -PI2_1, x, ALU.mult, ALU.add))
                link(v.scalar_tensor_tensor(r, k, -PI2_2, r, ALU.mult, ALU.add))

            s = small
            link(v.scalar_tensor_tensor(s("ar"), s("are"), -1.0, s("dt"), ALU.mult, ALU.mult))
            link(v.tensor_tensor(s("th"), s("ai"), s("dt"), ALU.mult))
            link(v.tensor_scalar(s("ars"), s("ar"), float(LA), None, ALU.mult))
            reduce_turns(s("r1"), s("th"), s("hk"))
            link(v.tensor_scalar(s("ra"), s("r1"), float(LA), None, ALU.mult))
            v.tensor_scalar(s("r1"), s("r1"), PI_IN, -PI_IN, ALU.min, ALU.max).then_inc(s_rates, 1)
            dve.wait_ge(s_rates, 1)
            reduce_turns(s("ra"), s("ra"), s("hk"))

            def phase(seg, col):
                link(v.tensor_scalar(seg, seg, c_col(col), PI_IN, ALU.add, ALU.min))

            link(v.tensor_tensor(ang[:].rearrange("p (h j) -> p h j", j=LJ), spread(s("ra"), [[1, NN], [0, LJ]]),
                                 spread(cst[:, C_J:C_J + LJ], [[0, NN], [1, LJ]]), ALU.mult))
            reduce_turns(ang[:], ang[:], turn[:], c_col(C_PHE))
            phase(ang[:], C_PHE + 1)
            v.tensor_scalar(ang[:], ang[:], -PI_IN, None, ALU.max).then_inc(s_ang, 1)

            make_hid(2, 0)
            g_len = NN * LA
            for part in range(2):
                link(v.tensor_tensor(ang_g[:, part * g_len:(part + 1) * g_len].rearrange("p (h a) -> p h a", a=LA),
                                     spread(s("r1"), [[1, NN], [0, LA]]),
                                     spread(cst[:, C_J:C_J + LA], [[0, NN], [1, LA]]), ALU.mult))
            for part, col in ((0, C_PHU), (1, C_PHV)):
                seg = slice(part * g_len, (part + 1) * g_len)
                reduce_turns(ang_g[:, seg], ang_g[:, seg], turn_g[:, seg], c_col(col))
                phase(ang_g[:, seg], col + 1)
            v.tensor_scalar(ang_g[:], ang_g[:], -PI_IN, None, ALU.max).then_inc(s_ang, 1)

            dve.wait_ge(s_exp1, 4)
            link(v.scalar_tensor_tensor(s("em"), s("ea"), 1.0, s("tnh"), ALU.add, ALU.mult))
            link(v.scalar_tensor_tensor(s("cm"), s("sh"), -2.0, s("sh"), ALU.mult, ALU.mult))
            link(v.tensor_tensor(s("zre"), s("ea"), s("cm"), ALU.mult))
            link(v.tensor_tensor(s("zre"), s("zre"), s("em"), ALU.add))
            link(v.tensor_tensor(s("zim"), s("ea"), s("sn"), ALU.mult))
            link(v.tensor_tensor(s("q1"), s("are"), s("are"), ALU.mult))
            link(v.tensor_tensor(s("den"), s("ai"), s("ai"), ALU.mult))
            link(v.tensor_tensor(s("den"), s("den"), s("q1"), ALU.add))
            link(v.reciprocal(s("rden"), s("den")))
            link(v.tensor_tensor(s("q1"), s("zim"), s("ai"), ALU.mult))
            link(v.tensor_tensor(s("q2"), s("zre"), s("are"), ALU.mult))
            link(v.tensor_tensor(s("q1"), s("q1"), s("q2"), ALU.subtract))
            link(v.tensor_tensor(s("q3"), s("zim"), s("are"), ALU.mult))
            link(v.tensor_tensor(s("q4"), s("zre"), s("ai"), ALU.mult))
            link(v.tensor_tensor(s("q3"), s("q3"), s("q4"), ALU.add))
            link(v.scalar_tensor_tensor(s("q1"), s("q1"), 2.0, s("rden"), ALU.mult, ALU.mult))
            link(v.scalar_tensor_tensor(s("q3"), s("q3"), -2.0, s("rden"), ALU.mult, ALU.mult))
            link(v.tensor_tensor(s("sre"), s("cr"), s("q1"), ALU.mult))
            link(v.tensor_tensor(s("q2"), s("ci"), s("q3"), ALU.mult))
            link(v.tensor_tensor(s("sre"), s("sre"), s("q2"), ALU.subtract))
            link(v.tensor_tensor(s("sim"), s("cr"), s("q3"), ALU.mult))
            link(v.tensor_tensor(s("q4"), s("ci"), s("q1"), ALU.mult))
            v.tensor_tensor(s("sim"), s("sim"), s("q4"), ALU.add).then_inc(s_cs, 1)

            split_b(2, 0)
            make_hid(3, 1)
            split_b(2, 1)
            make_hid(4, 0)
            dve.wait_ge(s_e, 2)
            with dve.Fori(0, 2) as i:
                split_b(i + 3, 0)
                make_hid(2 * i + 5, 1)
                split_b(i + 3, 1)
                make_hid(2 * i + 6, 0)
            split_b(5, 0)
            make_hid(9, 1)

            def copy_h(j, s_):
                if isinstance(j, int) and j < 2:
                    dve.wait_ge(wl_done, FC)
                else:
                    dve.wait_ge(down_used, j - 1)
                v.tensor_copy(hs[s_][:], hid[:, :, bass.ds(j * HT, HT)]).then_inc(hs_done, 1)

            def split_ha(j, s_):
                dve.wait_ge(hh_done, j + 1)
                v.tensor_tensor(ha_lo[s_][:], hid[:, 0, bass.ds(j * HT, HT)], ha_hi[s_][:].bitcast(F32),
                                ALU.subtract).then_inc(hl_done, 1)

            def split_a(j, s_):
                copy_h(j, s_)
                split_ha(j, s_)

            split_a(0, 0)
            for half in range(2):
                dve.wait_ge(silu_done, FC + half)
                v.tensor_tensor(hid[:, half, (FC - 1) * HT:FC * HT], silu[0][:, half * HT:(half + 1) * HT],
                                banks[:, 2 + half, :], ALU.mult).then_inc(hid_done, 1)
            dve.wait_ge(k_mm, 1)
            v.tensor_tensor(k_sb[:], banks[:, 6, 0:NN // 4 * LA].rearrange("p (h a) -> p h a", a=LA), skip_sb[:],
                            ALU.add).then_inc(k_ready, 1)
            with dve.Fori(0, 5) as i:
                split_a(2 * i + 1, 1)
                split_a(2 * i + 2, 0)

            dve.wait_ge(wdl_done, FC)

            def split_hb(j, s_):
                dve.wait_ge(hh_done, FC + j + 1)
                v.tensor_tensor(hb_lo[s_][:], hid[:, 1, bass.ds(j * HT, HT)], hb_hi[s_][:].bitcast(F32),
                                ALU.subtract).then_inc(hl_done, 1)
                dve.wait_ge(wdh_done, FC + j + 1)
                v.tensor_tensor(wd_lo[1 - s_][:], wd_raw[:, bass.ds(j, 1), :].rearrange("p o c -> p (o c)"),
                                wd_hi[1 - s_][:].bitcast(F32), ALU.subtract).then_inc(wdl_done, 1)

            def residual(half, c, bank):
                dve.wait_ge(y_done, half * KC + c + 1)
                ins = v.tensor_tensor(
                    x1[:, :, c, half * 2 * GB:(half + 1) * 2 * GB].rearrange("p n (q b) -> p q n b", b=PB),
                    banks[:, bank, :].rearrange("p (q n b) -> p q n b", n=NN, b=PB),
                    x_res[:, c, half * HT:(half + 1) * HT].rearrange("p (q n b) -> p q n b", n=NN, b=PB),
                    ALU.add)
                ins.then_inc(x1_done, 1)

            split_hb(0, 0)
            dve.wait_ge(td_done, 1)
            keep_own(td_mask[:], banks[:, 4, 0:NG * PB * NN], NG).then_inc(tdm_done, 1)
            dve.wait_ge(tdh_done, 1)
            v.tensor_tensor(td_lo[:], td_mask[:], td_hi[:].bitcast(F32), ALU.subtract).then_inc(tdl_done, 1)
            split_hb(1, 1)
            dve.wait_ge(d_xres, 16)
            for c in range(KC):
                split_hb(2 + c, c % 2)
                residual(0, c, c)
            split_hb(6, 0)
            with dve.Fori(0, 2) as i:
                split_hb(2 * i + 7, 1)
                split_hb(2 * i + 8, 0)
            for c in range(KC):
                residual(1, c, 4 + c)

            dve.wait_ge(d_pos, 16)

            def backwards(ap):
                return ap.rearrange("p (c l) -> p c l", l=P)[:, :, ::-1]

            def mask_sums(t, c0, c1):
                ls = slice(c0 * P, c1 * P)
                dve.wait_ge(conv_done, t + 1)
                if t >= 2:
                    dve.wait_ge(back_done, t - 1)
                v.scalar_tensor_tensor(conv_sb[t % 2][:, ls].rearrange("p (c l) -> p c l", l=P),
                                       backwards(pos_sb[:, ls]), len_f[:, 0:1], backwards(banks[:, t % 2, ls]),
                                       ALU.is_lt, ALU.mult).then_inc(sum_masked, 1)

            def add_sums(t, i, c0, c1, bank):
                dve.wait_ge(back_done, i + 1)
                x1n = x1[:, t * QN:(t + 1) * QN, c0:c1, :]
                v.tensor_tensor(x1n, banks[:, bank, :].rearrange("p (c n b) -> p n c b", c=KC, n=QN)[:, :, c0:c1, :],
                                x1n, ALU.add).then_inc(out_ready, 1)

            for t in range(STEPS - 1):
                mask_sums(t, 0, KC)
                add_sums(t, t, 0, KC, 2 + t % 2)
            for half in range(2):
                mask_sums(STEPS - 1, half * KC // 2, (half + 1) * KC // 2)
            for half in range(2):
                add_sums(STEPS - 1, STEPS - 1 + half, half * KC // 2, (half + 1) * KC // 2, 3 + half)

        @block.tensor
        def _(pe):
            mm = nc.tensor.matmul

            def three(dst, st_hi, st_lo, mv_hi, mv_lo, start, stop):
                mm(dst, st_hi, mv_hi, start=start, stop=False)
                mm(dst, st_hi, mv_lo, start=False, stop=False)
                return mm(dst, st_lo, mv_hi, start=False, stop=stop)

            def dense(s, half, gu):
                for k in range(KC):
                    c = gu * KC + k
                    hb = slice(half * HT, (half + 1) * HT)
                    last = three(banks[:, 4 * s + 2 * gu + half, :], w_hi[s][:, c, :], w_lo[s][:, c, :],
                                 x_hi[:, k, hb], x_lo[:, k, hb], k == 0, False)
                return last

            def lora(s):
                for half in range(2):
                    for gu in range(2):
                        for gg in range(2):
                            g = 2 * half + gg
                            last = three(banks[:, 4 * s + 2 * gu + half, gg * GT:(gg + 1) * GT],
                                         b_hi[s][:, g, gu * P:(gu + 1) * P], b_lo[s][:, g, gu * P:(gu + 1) * P],
                                         t_hi[:, gu, g * GT:(g + 1) * GT], t_lo[:, gu, g * GT:(g + 1) * GT],
                                         False, gg == 1)
                last.then_inc(gu_done, 1)

            pe.wait_ge(warm_ready, 1)
            for _ in range(WARM):
                last = mm(banks[:, 7, 0:P], warm[:], warm[:], start=True, stop=True)
            last.then_inc(warm_used, 1)
            for k in range(KC):
                for half in range(2):
                    hb = slice(half * HT, (half + 1) * HT)
                    pieces = sum(1 for piece in X_PIECES if piece[:2] <= (k, half * HT))

                    def products(w_, x_, start):
                        for gu in range(2):
                            ins = mm(banks[:, 2 * gu + half, :], w_[:, gu * KC + k, :], x_[:, k, hb], start=start,
                                     stop=False)
                        return ins

                    pe.wait_ge(first_hi if k == 0 else wh_done, 1)
                    pe.wait_ge(xh_done, pieces)
                    products(w_hi[0], x_hi, k == 0)
                    pe.wait_ge(first_lo if k == 0 else wl_done, 1)
                    products(w_lo[0], x_hi, False)
                    pe.wait_ge(xl_done, pieces)
                    last = products(w_hi[0], x_lo, False)
            last.then_inc(w_used, 1)
            for g in range(NG):
                if g < NG - 1:
                    pe.wait_ge(d_agu[g], 16 * GB)
                else:
                    pe.wait_ge(d_agu[g], 16 * (NB - A_SPLIT))
                    pe.wait_ge(d_agu_pool, 16 * (A_SPLIT - (NB - GB)))
                for gu in range(2):
                    cols = slice((2 * gu + g % 2) * PB * NN, (2 * gu + g % 2 + 1) * PB * NN)
                    for k in range(KC):
                        c = gu * KC + k
                        for q in range(GB // PB):
                            b0 = g * GB + q * PB
                            last = mm(banks[q * PB * RANK:(q + 1) * PB * RANK, 4 + g // 2, cols],
                                      agu_raw[:, b0:b0 + PB, :, c].rearrange("p b r -> p (b r)"),
                                      x_raw[:, k, b0 * NN:(b0 + PB) * NN],
                                      start=(k == 0), stop=(k == KC - 1))
                last.then_inc(la_done, 1)
            pe.wait_ge(wh_done, 2)
            pe.wait_ge(wl_done, 2)
            for gu in (1, 0):
                for half in range(2):
                    if gu == 0:
                        pe.wait_ge(tm_done, 2 * half + 2)
                    last = dense(1, half, gu)
            last.then_inc(w_used, 1)
            pe.wait_ge(th_done, 4)
            pe.wait_ge(tl_done, 4)
            for s in range(2):
                pe.wait_ge(bh_done, s + 1)
                pe.wait_ge(bl_done, s + 1)
                lora(s)

            def chunk(j, s):
                pe.wait_ge(wh_done, j + 1)
                pe.wait_ge(wl_done, j + 1)
                pe.wait_ge(hid_done, j - 1)
                for half in range(2):
                    for gu in range(2):
                        last = dense(s, half, gu)
                last.then_inc(w_used, 1)
                pe.wait_ge(bh_done, j + 1)
                pe.wait_ge(bl_done, j + 1)
                lora(s)

            with pe.Fori(0, 4) as i:
                chunk(2 * i + 2, 0)
                chunk(2 * i + 3, 1)
            chunk(10, 0)

            pe.wait_ge(s_e, 2)
            pe.wait_ge(hid_done, 10)
            for h in range(NN // 4):
                for t in range(4):
                    last = mm(banks[t * LJ:(t + 1) * LJ, 6, h * LA:(h + 1) * LA], ssm_e[:, t * 8 + h, :],
                              ssm_g[:, t * 8 + h, :], start=True, stop=True)
            last.then_inc(k_mm, 1)

            def down(s, half_bank, order, mv_hi, mv_lo, s_w, start, waits=()):
                for n, c in enumerate(order):
                    if n < len(waits) and waits[n] is not None:
                        pe.wait_ge(*waits[n])
                    last = three(banks[:, half_bank + c, :], wd_hi[s_w][:, c * P:(c + 1) * P],
                                 wd_lo[s_w][:, c * P:(c + 1) * P], mv_hi, mv_lo, start, False)
                last.then_inc(down_used, 1)

            def unit_a(j, s, first=False, final=False):
                pe.wait_ge(ad_done, j + 1)
                pe.wait_ge(hs_done, j + 1)
                for g in range(NG):
                    for q in range(GB // PB):
                        b0 = g * GB + q * PB
                        last = mm(banks[q * PB * RANK:(q + 1) * PB * RANK, 4, g * PB * NN:(g + 1) * PB * NN],
                                  ad_rows[s][:, b0 * RANK:(b0 + PB) * RANK],
                                  hs[s][:, g // 2, (b0 * NN) % HT:(b0 * NN) % HT + PB * NN],
                                  start=first and g == 0, stop=final and g == NG - 1)
                if final:
                    last.then_inc(td_done, 1)
                pe.wait_ge(hh_done, j + 1)
                pe.wait_ge(hl_done, j + 1)
                pe.wait_ge(wdh_done, j + 1)
                pe.wait_ge(wdl_done, j + 1)
                waits = ((hid_done, FC), None, (hid_done, FC + 1)) if first else ()
                down(s, 0, (0, 2, 1, 3), ha_hi[s][:], ha_lo[s][:], s, first, waits)

            unit_a(0, 0, first=True)
            with pe.Fori(0, 4) as i:
                unit_a(2 * i + 1, 1)
                unit_a(2 * i + 2, 0)
            unit_a(9, 1)
            unit_a(10, 0, final=True)

            def unit_b(j, s, first=False):
                pe.wait_ge(hh_done, FC + j + 1)
                pe.wait_ge(hl_done, FC + j + 1)
                pe.wait_ge(wdh_done, FC + j + 1)
                pe.wait_ge(wdl_done, FC + j + 1)
                waits = ((k_ready, 1), None, (tdm_done, 1)) if first else ()
                down(s, 4, (2, 3, 0, 1), hb_hi[s][:], hb_lo[s][:], 1 - s, first, waits)

            def lora_down(half):
                for c in range(KC):
                    for gg in range(2):
                        g = 2 * half + gg
                        if half == 0 and c == 0:
                            pe.wait_ge(bdh_done, NG)
                            pe.wait_ge(bdl_done, NG)
                        last = three(banks[:, 4 * half + c, gg * GT:(gg + 1) * GT], bd_hi[:, g, c * P:(c + 1) * P],
                                     bd_lo[:, g, c * P:(c + 1) * P], td_hi[:, g * GT:(g + 1) * GT],
                                     td_lo[:, g * GT:(g + 1) * GT], False, gg == 1)
                    last.then_inc(y_done, 1)

            unit_b(0, 0, first=True)
            pe.wait_ge(tdh_done, 1)
            pe.wait_ge(tdl_done, 1)
            lora_down(0)
            with pe.Fori(0, 5) as i:
                unit_b(2 * i + 1, 1)
                unit_b(2 * i + 2, 0)
            lora_down(1)

            def bring_back(t, i, c0, c1, bank):
                pe.wait_ge(sum_masked, i + 1)
                if t >= 2:
                    pe.wait_ge(out_ready, t - 1)
                for c in range(c0, c1):
                    last = nc.tensor.transpose(banks[:, bank, c * P:(c + 1) * P],
                                               conv_sb[t % 2][:, c * P:(c + 1) * P], eye_sb[:])
                last.then_inc(back_done, 1)

            def conv(t):
                q, turn_ = t % NQ, t // NQ
                pe.wait_ge(d_t[q], 16 * (turn_ + 1))
                if t >= 2:
                    pe.wait_ge(sum_masked, t - 1)
                for c in range(KC):
                    if t == 0:
                        pe.wait_ge(x1_done, KC + c + 1)
                    for n in range(QN):
                        last = mm(banks[n * NB:(n + 1) * NB, t % 2, c * P:H], x1[:, t * QN + n, c, :],
                                  toep[q][:, n, 0:H - c * P], start=(c == 0), stop=(c == KC - 1))
                    if t > 0 and c == 1:
                        bring_back(t - 1, t - 1, 0, KC, 2 + (t - 1) % 2)
                last.then_inc(conv_done, 1)

            pe.wait_ge(d_small, 48)
            for t in range(STEPS):
                conv(t)
            for half in range(2):
                bring_back(STEPS - 1, STEPS - 1 + half, half * KC // 2, (half + 1) * KC // 2, 3 + half)


def kernel(x, itok_B_2_6, itok_B_8_3872, L0_cond_W_gate, L0_cond_W_up, L0_cond_W_down, L0_cond_A_gate,
           L0_cond_B_gate, L0_cond_A_up, L0_cond_B_up, L0_cond_A_down, L0_cond_B_down, L1_cond_log_dt,
           L1_cond_C, L1_cond_log_A_real, L1_cond_A_imag, L1_cond_D):
    import concourse.bacc as bacc
    from concourse.bass_utils import run_bass_kernel_spmd

    def pad_f(a, axis, size=FC * P):
        width = [(0, 0)] * a.ndim
        width[axis] = (0, size - a.shape[axis])
        return np.pad(a, width)

    x = np.asarray(x)
    x_t = x.reshape(NB // PB, PB, NN, KC, P).transpose(4, 3, 0, 2, 1).reshape(P, KC, TOK)
    w = np.stack([pad_f(np.asarray(a), 0) for a in (L0_cond_W_gate, L0_cond_W_up)])
    w_gu = w.reshape(2, FC, P, KC, P).transpose(1, 4, 0, 3, 2).reshape(FC, P, 2 * KC, P)
    w_d = pad_f(np.asarray(L0_cond_W_down), 1).T.reshape(FC, P, KC, P)[..., ::-1].transpose(1, 0, 2, 3)
    w_d = w_d.reshape(P, FC, H)
    a = np.stack([np.asarray(L0_cond_A_gate)[0], np.asarray(L0_cond_A_up)[0]])
    a_gu = a.reshape(2, NAD, RANK, KC, P).transpose(1, 4, 2, 0, 3).reshape(NAD, P, RANK * 2 * KC)
    a_d = pad_f(np.asarray(L0_cond_A_down)[0], 2).reshape(NAD, RANK, FC, P).transpose(0, 3, 2, 1)
    a_d = a_d.reshape(NAD, P, FC * RANK)
    b = np.stack([pad_f(np.asarray(m)[0], 1, 2 * NPART * P) for m in (L0_cond_B_gate, L0_cond_B_up)])
    b_gu = b.reshape(2, NAD, NPART, 2, P, RANK).transpose(2, 1, 5, 3, 0, 4).reshape(NPART * NAD * RANK, 4 * P)
    b_d = np.asarray(L0_cond_B_down)[0].transpose(0, 2, 1).reshape(NAD * RANK, KC, P)[..., ::-1]
    b_d = b_d.reshape(NAD * RANK, H)
    idx = np.asarray(itok_B_2_6)
    ints = np.concatenate([np.tile(np.asarray(itok_B_8_3872), QN)[:, None],
                           np.repeat(idx.reshape(NG, GB).T, RANK, axis=0)], axis=1)
    c = np.asarray(L1_cond_C)
    rates = np.stack([np.tile(np.asarray(L1_cond_log_dt), (MODES, 1)), np.asarray(L1_cond_log_A_real).T,
                      np.asarray(L1_cond_A_imag).T, c[:, :, 0].T, c[:, :, 1].T], axis=1)
    params = np.concatenate([rates, rates], axis=0).reshape(P, 5 * NN)
    skip = np.zeros((4, LJ, NN // 4, LA), np.float32)
    skip[:, 0, :, 0] = np.asarray(L1_cond_D).reshape(4, NN // 4)
    skip = skip.reshape(P, NN // 4, LA)

    nc = bacc.Bacc("TRN2", target_bir_lowering=False, num_devices=1)
    arrays, args = {}, []
    for name, v in (("x_t", x_t), ("x_rev", x_t[::-1]), ("w_gu", w_gu), ("w_d", w_d), ("a_gu", a_gu),
                    ("a_d", a_d), ("b_gu", b_gu), ("b_d", b_d), ("idx_row", idx.reshape(1, NB)), ("ints", ints),
                    ("params", params), ("skip", skip), ("eye", np.eye(P, dtype=np.float32)),
                    ("pos", np.tile(np.arange(H, dtype=np.float32), (P, 1))),
                    ("consts", constants())):
        v = np.ascontiguousarray(v)
        arrays[name] = v
        args.append(nc.dram_tensor(name, v.shape, mybir.dt.from_np(v.dtype), kind="ExternalInput").ap())
    out = nc.dram_tensor("out", (P, NN, KC, NB), F32, kind="ExternalOutput").ap()
    program(nc, *args, out)
    r = run_bass_kernel_spmd(nc, [arrays], core_ids=[0])
    y = r.results[0]["out"][::-1]
    return y.transpose(3, 1, 2, 0).reshape(NB, NN, H)
```
